# Optimizing a Trainium2 kernel written in Bass

```python
import numpy as np
import jax
import jax.numpy as jnp

def _softmax(x, axis=-1):
    return jax.nn.softmax(x, axis=axis)

def _gelu(x):
    return jax.nn.gelu(x, approximate=True)

def _silu(x):
    return jax.nn.silu(x)

def _sigmoid(x):
    return jax.nn.sigmoid(x)

def _layernorm(x, axis=-1, eps=1e-05):
    m = jnp.mean(x, axis=axis, keepdims=True)
    v = jnp.var(x, axis=axis, keepdims=True)
    return (x - m) / jnp.sqrt(v + eps)

def _scatter_add(tgt, idx, src, axis=0):
    return tgt.at[idx].add(src)

def _segment_sum(src, seg, n):
    return jax.ops.segment_sum(src, seg, n)
kernel_name = 'mk_xattn_seq_d1_seqx_r2_8eb94e'

def setup_inputs(seed: int=0):
    np.random.seed(seed)
    _w = jnp.asarray

    def _rec_inputs():
        import jax
        import jax.numpy as jnp
        _rk = jax.random.key(seed)
        x = -0.000125 + 0.9999 * jax.random.normal(jax.random.fold_in(_rk, 1), (16, 256, 1024), jnp.float32)
        _lenS = 256 - jax.random.randint(jax.random.fold_in(_rk, 7), (16,), 0, max(1, 256 // 4) + 1, jnp.int32)
        _lenS2 = 256 - jax.random.randint(jax.random.fold_in(_rk, 8), (16,), 0, max(1, 256 // 4) + 1, jnp.int32)
        _ctx_1024P = jax.random.normal(jax.random.fold_in(_rk, 11), (16, 16, 512), jnp.float32)
        _ctx_1024c = jax.random.dirichlet(jax.random.fold_in(_rk, 511), 0.3 * jnp.ones((16,), jnp.float32), (16, 256))
        _ctx_1024t = jnp.einsum('bsk,bkd->bsd', _ctx_1024c, _ctx_1024P)
        _ctx_1024t = _ctx_1024t * jax.lax.rsqrt(jnp.mean(jnp.square(_ctx_1024t)) + 1e-12) * 0.953939
        ctx_1024 = 4.13588e-05 + 0.999923 * (_ctx_1024t + 0.3 * jax.random.normal(jax.random.fold_in(_rk, 611), (16, 256, 512), jnp.float32))
        return (x, ctx_1024)
    x, ctx_1024 = _rec_inputs()

    def _L0_xattn_setup():
        import jax, jax.numpy as jnp
        import numpy as np
        EPS = 1e-06

        def _rmsnorm(x, w):
            var = jnp.mean(jnp.square(x), axis=-1, keepdims=True)
            return x * jax.lax.rsqrt(var + EPS) * w
        key = jax.random.key(seed)
        ks = jax.random.split(key, 6)
        B, N, M = (4, 2048, 1024)
        d_model, memory_dim = (1024, 512)
        hidden_states = jax.random.normal(ks[0], (B, N, d_model), dtype=jnp.float32)
        memory = jax.random.normal(ks[1], (B, M, memory_dim), dtype=jnp.float32)
        W_mem = jax.random.normal(ks[2], (d_model, memory_dim), dtype=jnp.float32) / np.sqrt(memory_dim)
        W_gate = jax.random.normal(ks[3], (d_model, 2 * d_model), dtype=jnp.float32) / np.sqrt(2 * d_model)
        b_gate = jax.random.normal(ks[4], (d_model,), dtype=jnp.float32) * 0.01
        norm_w = jnp.ones((d_model,), dtype=jnp.float32)
        return {'hidden_states': hidden_states, 'memory': memory, 'W_mem': W_mem, 'W_gate': W_gate, 'b_gate': b_gate, 'norm_w': norm_w}
    _L0_xattn_all = _L0_xattn_setup()
    _L0_xattn_in = {k: v for k, v in _L0_xattn_all.items() if k in ('W_mem', 'W_gate', 'b_gate', 'norm_w')}
    del _L0_xattn_all
    return {'x': x, 'ctx_1024': ctx_1024, 'L0_xattn_W_mem': _L0_xattn_in['W_mem'], 'L0_xattn_W_gate': _L0_xattn_in['W_gate'], 'L0_xattn_b_gate': _L0_xattn_in['b_gate'], 'L0_xattn_norm_w': _L0_xattn_in['norm_w']}

def reference(x, ctx_1024, L0_xattn_W_mem, L0_xattn_W_gate, L0_xattn_b_gate, L0_xattn_norm_w):
    import jax
    import jax.numpy as jnp

    def _L0_xattn_ref(hidden_states, memory, W_mem, W_gate, b_gate, norm_w):
        import jax, jax.numpy as jnp
        import numpy as np
        EPS = 1e-06

        def _rmsnorm(x, w):
            var = jnp.mean(jnp.square(x), axis=-1, keepdims=True)
            return x * jax.lax.rsqrt(var + EPS) * w
        D = hidden_states.shape[-1]
        memory_proj = jnp.einsum('bme,de->bmd', memory, W_mem)
        scores = jnp.einsum('bnd,bmd->bnm', hidden_states, memory_proj) / jnp.sqrt(jnp.float32(D))
        attn = jax.nn.softmax(scores, axis=-1)
        memory_context = jnp.einsum('bnm,bmd->bnd', attn, memory_proj)
        gate_input = jnp.concatenate([hidden_states, memory_context], axis=-1)
        gate = jax.nn.sigmoid(jnp.einsum('bnf,df->bnd', gate_input, W_gate) + b_gate)
        fused = hidden_states + gate * memory_context
        return _rmsnorm(fused, norm_w)
    x = _L0_xattn_ref(x, ctx_1024, L0_xattn_W_mem, L0_xattn_W_gate, L0_xattn_b_gate, L0_xattn_norm_w)
    return x

_drawn_inputs = setup_inputs


def setup_inputs(seed=0):
    import zlib

    import numpy as np

    out = dict(_drawn_inputs(seed))
    spreads = {'L0_xattn_norm_w': (1.0, 0.2)}
    factors = {'L0_xattn_b_gate': 50.264}
    for name, (base, spread) in spreads.items():
        noise = np.random.default_rng([zlib.crc32(name.encode()), seed]).standard_normal(out[name].shape)
        drawn = base * np.exp(spread * noise) if base else spread * noise
        out[name] = jnp.asarray(drawn.astype(out[name].dtype))
    for name, factor in factors.items():
        out[name] = (out[name] * factor).astype(out[name].dtype)
    return out
```

```python
from contextlib import ExitStack

import concourse.bass as bass
from concourse import mybir

F32 = mybir.dt.float32
F32R = mybir.dt.float32r
ACT = mybir.ActivationFunctionType
ALU = mybir.AluOpType
AX = mybir.AxisListType

PART = 128
BLK = 32
QUADS = PART // BLK
BANK = 512
EPS = 1e-6


def build(nc, x, ctx_in, w_mem, w_gate, b_gate, norm_w, out):
    B, N, D = x.shape
    M, E = ctx_in.shape[1:]
    NB, MB = N // PART, M // PART
    KD, KE = D // PART, E // PART
    HALVES = D // BANK
    DQ, EQ = D // QUADS, E // QUADS
    SCALE = 1.0 / float(D) ** 0.5
    DMA = 16

    with ExitStack() as ctx:
        def sem(name):
            return ctx.enter_context(nc.semaphore(name))

        def const(name, shape, dtype):
            return ctx.enter_context(nc.sbuf_tensor(name, shape, dtype))

        wt_h, wt_l = (const(f"wt_{s}", [PART, KE, D], F32R) for s in "hl")
        k_h, k_l = (const(f"k_{s}", [PART, KE, D], F32R) for s in "hl")
        g1_h = const("g1_h", [PART, KD, D], F32R)
        g1_l_mem = const("g1_l_mem", [PART, KD * D], F32)
        bias = const("bias", [PART, D], F32)
        norm = const("norm", [PART, D], F32)
        ident = const("ident", [PART, PART], F32)
        ident_r = const("ident_r", [PART, PART], F32R)
        stat = const("stat", [PART, 32], F32)
        KB = 1024
        work = const("work", [PART, 68 * KB // 4], F32)

        def at(name, shape, dtype, mem, kb):
            return nc.alloc_sbuf_tensor_at(name, shape, dtype, offset=nc.lookup_mloc(mem).addr + kb * KB)

        g1_l = at("g1_l", [PART, KD, D], F32R, g1_l_mem, 0)
        wn_h = at("wn_h", [PART, KD, E], F32R, g1_l_mem, 0)
        wn_l = at("wn_l", [PART, KD, E], F32R, g1_l_mem, 16)
        xt_h = at("xt_h", [PART, KD, N], F32R, work, 0)
        xt_l = at("xt_l", [PART, KD, N], F32R, work, 8)
        p_h = at("p_h", [PART, MB, D], F32R, work, 16)
        p_l = at("p_l", [PART, MB, D], F32R, work, 24)
        g2_h = at("g2_h", [PART, 2, 4, DQ], F32R, work, 16)
        g2_l = at("g2_l", [PART, 2, 4, DQ], F32R, work, 24)
        ct_h = at("ct_h", [PART, KE, M], F32R, work, 32)
        ct_l = at("ct_l", [PART, KE, M], F32R, work, 36)
        pt_h = at("pt_h", [PART, 2, 2, M], F32R, work, 32)
        pt_l = at("pt_l", [PART, 2, 2, M], F32R, work, 36)
        prob = at("prob", [PART, NB, M], F32, work, 32)
        at_h = at("at_h", [PART, MB, N], F32R, work, 34)
        at_l = at("at_l", [PART, MB, N], F32R, work, 36)
        ctt_h = at("ctt_h", [PART, KE, MB * PART], F32R, work, 40)
        ctt_l = at("ctt_l", [PART, KE, MB * PART], F32R, work, 44)
        xrow = [at(f"xrow{i}", [PART, D], F32, work, 48 + 4 * i) for i in range(NB)]
        gate = at("gate", [PART, D], F32, work, 56)
        stage = at("stage", [PART, D], F32, work, 60)
        turned = at("turned", [PART, D], F32, work, 64)
        ring = [stage] + [at(f"ring{i}", [PART, D], F32, work, 48 + 4 * (i - 1)) for i in range(1, 4)]
        turned2 = [turned, at("turned_b", [PART, D], F32, work, 40)]

        negmax, rowmax = stat[:, 0:NB], stat[:, 2:2 + NB]
        rowsum, rowinv = stat[:, 4:4 + NB], stat[:, 6:6 + NB]
        meansq, guarded, rstd = stat[:, 8:8 + NB], stat[:, 10:10 + NB], stat[:, 12:12 + NB]
        minus_half, eps = stat[:, 14:15], stat[:, 15:16]

        psum = ctx.enter_context(nc.psum_tensor("psum", [PART, 8, BANK], F32))

        def bank(i):
            return psum[:, i, :]

        ring_in = [sem(f"ring{i}_in") for i in range(4)]
        consts_in = sem("consts_in")
        xs_in, cs_in, cn_in = sem("xs_in"), sem("cs_in"), sem("cn_in")
        xrow_in = [sem(f"xrow{i}_in") for i in range(NB)]
        out_done = [sem(f"out{i}_done") for i in range(NB)]
        ident_done, ident_r_done = sem("ident_done"), sem("ident_r_done")
        item_turned = sem("item_turned")
        item_h = sem("item_h")
        item_ready = sem("item_ready")
        k_high, k_ready = sem("k_high"), sem("k_ready")
        g2_used = sem("g2_used")
        xs_moved, cs_moved = sem("xs_moved"), sem("cs_moved")
        xt_high, xt_ready, xt_used = sem("xt_high"), sem("xt_ready"), sem("xt_used")
        ct_high, ct_ready = sem("ct_high"), sem("ct_ready")
        cn_high, cn_ready = sem("cn_high"), sem("cn_ready")
        p_mm, p_high, p_ready = sem("p_mm"), sem("p_high"), sem("p_ready")
        pth_mm, pth_ready = sem("pth_mm"), sem("pth_ready")
        ptl_mm, ptl_ready = sem("ptl_mm"), sem("ptl_ready")
        pt_used = sem("pt_used")
        max_done, negmax_done = sem("max_done"), sem("negmax_done")
        exp_done, inv_done, prob_ready = sem("exp_done"), sem("inv_done"), sem("prob_ready")
        at_mm, at_high, at_ready = sem("at_mm"), sem("at_high"), sem("at_ready")
        tt_mm, tt_high, tt_ready = sem("tt_mm"), sem("tt_high"), sem("tt_ready")
        m_mm, gate_mm = sem("m_mm"), sem("gate_mm")
        z_ready, tanh_done, gm_ready, f_ready = sem("z_ready"), sem("tanh_done"), sem("gm_ready"), sem("f_ready")
        sq_done, guarded_done, rstd_ready, row_ready = (sem("sq_done"), sem("guarded_done"), sem("rstd_ready"),
                                                       sem("row_ready"))

        items = [("wn", i) for i in range(4)] + [("g2", 0), ("g2", 1)]
        for i in range(4):
            items += [("wt", i), ("g2", i + 2)]
        items += [("ct", 0), ("g2", 6), ("xt", 0), ("g2", 7), ("xt", 1)]
        n_before_k = len(items)
        items += [("g1", i) for i in range(8)]
        pos = {item: n for n, item in enumerate(items)}
        dmas = {"wn": 2 * QUADS, "g2": 2 * QUADS, "g1": 2 * QUADS, "wt": QUADS, "ct": QUADS, "xt": QUADS}

        def turned_count(n):
            return n - 3

        def ring_count(n):
            return DMA * sum(dmas[items[i][0]] for i in range(n % 4, n + 1, 4))

        def blocks(mat, rows0, n_rows, col0, n_cols):
            return mat[rows0:rows0 + n_rows, col0:col0 + n_cols].rearrange("(i c) f -> c i f", c=BLK)

        def on_stage(stage_buf, q, i_count):
            return stage_buf[BLK * q:BLK * q + BLK, :].rearrange("c (i f) -> c i f", i=i_count)

        def load_item(sp, n):
            kind, i = items[n]
            buf, done = ring[n % 4], ring_in[n % 4]
            for q in range(QUADS):
                if kind == "wn":
                    for kk in range(2):
                        r0 = DQ * q + BLK * (2 * i + kk)
                        sp.dma_start(buf[BLK * q:BLK * q + BLK, E * kk:E * kk + E],
                                     w_mem[r0:r0 + BLK, :]).then_inc(done, DMA)
                elif kind in ("g1", "g2"):
                    g, h = i // 2, i % 2
                    col = (D if kind == "g2" else 0) + DQ * q + PART * h
                    for part in range(2):
                        sp.dma_start(on_stage(buf, q, 8)[:, 4 * part:4 * part + 4, :],
                                     blocks(w_gate, 256 * g + 128 * part, 128, col, PART)).then_inc(done, DMA)
                elif kind == "wt":
                    sp.dma_start(on_stage(buf, q, 8), blocks(w_mem, 256 * i, 256, EQ * q, EQ)).then_inc(done, DMA)
                elif kind == "ct":
                    sp.dma_start(on_stage(buf, q, 8), blocks(ctx_in[0], 0, M, EQ * q, EQ)).then_inc(done, DMA)
                else:
                    sp.dma_start(on_stage(buf, q, 4),
                                 blocks(x[0], PART * i, PART, DQ * q, DQ)).then_inc(done, DMA)

        def turn_views(src, dst, i_count):
            k = D // (i_count * BLK)
            return (src[:, :].rearrange("p (i k r) -> p k i r", i=i_count, k=k),
                    dst[:, :].rearrange("p (k i c) -> p k i c", k=k, i=i_count))

        def item_parts(n):
            kind, i = items[n]
            src = turned2[n % 2]
            if kind == "wn":
                return (ring[n % 4][:, :].rearrange("p (k e) -> p k e", k=2),
                        wn_h[:, 2 * i:2 * i + 2, :], wn_l[:, 2 * i:2 * i + 2, :])
            if kind == "xt":
                v = src[:, :].rearrange("p (k n) -> p k n", k=KD)
                return v, xt_h[:, :, PART * i:PART * i + PART], xt_l[:, :, PART * i:PART * i + PART]
            v = src[:, :].rearrange("p (k n) -> p k n", k=4)
            if kind == "g2":
                return v, g2_h[:, i % 2], g2_l[:, i % 2]
            if kind == "wt":
                return (src[:, :].rearrange("p (e k r) -> p e k r", e=KE, k=KD),
                        *(w[:, :, :].rearrange("p e (k q r) -> p e k q r", k=KD, q=QUADS)[:, :, :, i, :]
                          for w in (wt_h, wt_l)))
            if kind == "ct":
                return v, ct_h[:, :, :], ct_l[:, :, :]
            g, h = i // 2, i % 2
            return (v, g1_h[:, 4 * h:4 * h + 4, 256 * g:256 * g + 256],
                    g1_l[:, 4 * h:4 * h + 4, 256 * g:256 * g + 256])

        def p_tile(t):
            return t % 2, t // 2, (0, 1, 4, 5)[t]

        def p_cols(buf, mb, j):
            return buf[:, mb, BANK * j:BANK * j + BANK]

        def p_natural(buf, mb, half):
            return buf[:, mb, :].rearrange("p (k q r) -> p q k r", k=KD, q=QUADS)[:, 2 * half:2 * half + 2]

        PT_BANKS = [(6, 7), (0, 1)]
        block = ctx.enter_context(nc.Block())

        @block.sync
        def _(sp):
            for n in range(4):
                load_item(sp, n)
            sp.dma_start(bias[:, :], b_gate.rearrange("(a d) -> a d", a=1).to_broadcast((PART, D))
                         ).then_inc(consts_in, DMA)
            sp.dma_start(norm[:, :], norm_w.rearrange("(a d) -> a d", a=1).to_broadcast((PART, D))
                         ).then_inc(consts_in, DMA)
            for n in range(4, len(items)):
                if n < 8:
                    sp.wait_ge(item_ready, n - 3)
                else:
                    sp.wait_ge(item_turned, turned_count(n - 4))
                load_item(sp, n)

            def load_c_rows(b, first):
                if first:
                    sp.wait_ge(item_turned, turned_count(24))
                else:
                    sp.wait_ge(cs_moved, b)
                sp.dma_start(stage[:, :].rearrange("p (m e) -> p m e", m=MB),
                             ctx_in[bass.ds(b, 1)].rearrange("a (m p) e -> p (a m) e", p=PART)).then_inc(cn_in, DMA)

            def load_x_rows(b, first):
                for nb in range(NB):
                    if first:
                        sp.wait_ge(item_turned, turned_count(len(items) - 1))
                    else:
                        sp.wait_ge(out_done[nb], DMA * b)
                    sp.dma_start(xrow[nb][:, :],
                                 x[bass.ds(b, 1), PART * nb:PART * nb + PART, :].rearrange("a p d -> p (a d)")
                                 ).then_inc(xrow_in[nb], DMA)

            def store_rows(b):
                for nb in range(NB):
                    sp.wait_ge(row_ready, 2 * b + nb + 1)
                    sp.dma_start(out[bass.ds(b, 1), PART * nb:PART * nb + PART, :].rearrange("a p d -> p (a d)"),
                                 xrow[nb][:, :]).then_inc(out_done[nb], DMA)

            load_c_rows(0, True)
            load_x_rows(0, True)
            with sp.Fori(1, B) as b:
                for nb in range(NB):
                    if nb == 0:
                        sp.wait_ge(cn_ready, b)
                    else:
                        sp.wait_ge(xs_moved, 2 * b - 1)
                    for q in range(QUADS):
                        sp.dma_start(on_stage(stage, q, 4),
                                     x[bass.ds(b, 1), PART * nb:PART * nb + PART, DQ * q:DQ * q + DQ].rearrange(
                                         "a (i c) f -> c (a i) f", c=BLK)).then_inc(xs_in, DMA)
                sp.wait_ge(xs_moved, 2 * b)
                for q in range(QUADS):
                    sp.dma_start(on_stage(stage, q, 8),
                                 ctx_in[bass.ds(b, 1), :, EQ * q:EQ * q + EQ].rearrange(
                                     "a (i c) f -> c (a i) f", c=BLK)).then_inc(cs_in, DMA)
                load_c_rows(b, False)
                store_rows(b - 1)
                load_x_rows(b, False)
            store_rows(B - 1)
            for nb in range(NB):
                sp.wait_ge(out_done[nb], DMA * B)

        @block.gpsimd
        def _(pool):
            pool.memset(ident[:, :], 0.0).then_inc(ident_done, 1)
            pool.memset(minus_half, -0.5).then_inc(ident_done, 1)
            pool.memset(eps, EPS).then_inc(ident_done, 1)
            pool.wait_ge(ident_done, 3)
            pool.affine_select(out=ident[:, :], in_=ident[:, :], compare_op=ALU.not_equal, fill=1.0, base=0,
                               pattern=[[-1, PART]], channel_multiplier=1).then_inc(ident_done, 1)

            def batch(b):
                for nb in range(NB):
                    done = 2 * b + nb + 1
                    pool.wait_ge(sq_done, done)
                    pool.tensor_tensor(guarded[:, nb:nb + 1], meansq[:, nb:nb + 1], eps,
                                       ALU.add).then_inc(guarded_done, 1)
                    pool.wait_ge(guarded_done, done)
                    pool.tensor_tensor(rstd[:, nb:nb + 1], guarded[:, nb:nb + 1], minus_half,
                                       ALU.pow).then_inc(rstd_ready, 1)

            batch(0)
            with pool.Fori(1, B) as b:
                batch(b)

        @block.scalar
        def _(act):
            def copy(dst, src):
                return nc.scalar.activation(dst, src, ACT.Copy)

            def item(n):
                kind, i = items[n]
                src, high, _ = item_parts(n)
                if kind == "wn":
                    act.wait_ge(ring_in[n % 4], ring_count(n))
                else:
                    act.wait_ge(item_turned, turned_count(n))
                if kind == "g2" and i >= 2:
                    act.wait_ge(g2_used, i - 1)
                copy(high, src).then_inc(item_h, 1)

            def k_part(g):
                act.wait_ge(g2_used, 2 * g + 2)
                copy(k_h[:, :, DQ * g:DQ * g + DQ],
                     psum[:, 4 * (g % 2):4 * (g % 2) + 4, 0:DQ]).then_inc(k_high, 1)

            for n in range(n_before_k):
                item(n)
                if items[n] == ("g2", 3):
                    act.wait_ge(ident_done, 4)
                    copy(ident_r[:, :], ident[:, :]).then_inc(ident_r_done, 1)
                if items[n][0] == "g2" and items[n][1] % 2 and items[n][1] >= 3:
                    k_part((items[n][1] - 3) // 2)
            k_part(3)
            for i in range(4):
                item(pos["g1", i])

            def batch(b, first, last):
                for t in range(4):
                    mb, j, bk = p_tile(t)
                    act.wait_ge(p_mm, 4 * b + t + 1)
                    copy(p_cols(p_h, mb, j), bank(bk)).then_inc(p_high, 1)
                for g in range(4):
                    act.wait_ge(pth_mm, 4 * b + g + 1)
                    if g >= 2:
                        act.wait_ge(pt_used, 4 * b + g - 1)
                    copy(pt_h[:, g % 2].rearrange("p k m -> p (k m)"),
                         bank(PT_BANKS[g % 2][0])).then_inc(pth_ready, 1)
                act.wait_ge(negmax_done, b + 1)
                for nb in range(NB):
                    nc.scalar.activation(prob[:, nb, :], psum[:, 2 + nb, 0:M], ACT.Exp, bias=negmax[:, nb:nb + 1],
                                         scale=SCALE, accum_out=rowsum[:, nb:nb + 1]).then_inc(exp_done, 1)
                if first:
                    for i in range(4, 8):
                        item(pos["g1", i])
                    act.wait_ge(item_ready, len(items))
                act.wait_ge(cn_in, DMA * (b + 1))
                copy(ctt_h[:, :, :].rearrange("p j (m c) -> p j m c", m=MB),
                     stage[:, :].rearrange("p (m j c) -> p j m c", m=MB, j=KE)).then_inc(cn_high, 1)
                act.wait_ge(at_mm, b + 1)
                copy(at_h[:, :, :].rearrange("p m n -> p (m n)"), bank(4)).then_inc(at_high, 1)
                for i in range(2):
                    act.wait_ge(tt_mm, 2 * b + i + 1)
                    copy(ctt_h[:, 2 * i:2 * i + 2, :].rearrange("p j n -> p (j n)"),
                         bank(6 + i)).then_inc(tt_high, 1)
                if not last:
                    act.wait_ge(xt_used, b + 1)
                    for nb in range(NB):
                        act.wait_ge(xs_moved, 2 * b + nb + 1)
                        copy(xt_h[:, :, PART * nb:PART * nb + PART],
                             turned[:, :].rearrange("p (k n) -> p k n", k=KD)).then_inc(xt_high, 1)
                    act.wait_ge(cs_moved, b + 1)
                    act.wait_ge(m_mm, b + 1)
                    copy(ct_h[:, :, :], turned[:, :].rearrange("p (k n) -> p k n", k=KE)).then_inc(ct_high, 1)
                for nb in range(NB):
                    done = 2 * b + nb + 1
                    act.wait_ge(z_ready, done)
                    nc.scalar.activation(gate[:, :], gate[:, :], ACT.Tanh, scale=0.5).then_inc(tanh_done, 1)
                    act.wait_ge(f_ready, done)
                    nc.scalar.activation(turned[:, :], xrow[nb][:, :], ACT.Square, scale=SCALE,
                                         accum_out=meansq[:, nb:nb + 1]).then_inc(sq_done, 1)

            batch(0, True, False)
            with act.Fori(1, B - 1) as b:
                batch(b, False, False)
            batch(B - 1, False, True)

        @block.vector
        def _(dve):
            def low(dst, src, high):
                return nc.vector.tensor_tensor(dst, src, high.bitcast(F32), ALU.subtract)

            def turn(n):
                kind, i = items[n]
                dve.wait_ge(ring_in[n % 4], ring_count(n))
                if n >= 6:
                    dve.wait_ge(item_ready, n - 1)
                src, dst = turn_views(ring[n % 4], turned2[n % 2], 4 if kind == "xt" else 8)
                nc.vector.transpose(dst, src).then_inc(item_turned, 1)

            def cut(n):
                kind, i = items[n]
                src, high, lo = item_parts(n)
                dve.wait_ge(item_h, n + 1)
                if kind == "g1":
                    dve.wait_ge(g2_used, 8)
                low(lo, src, high).then_inc(item_ready, 1)

            def k_part(g):
                dve.wait_ge(k_high, g + 1)
                cols = slice(DQ * g, DQ * g + DQ)
                low(k_l[:, :, cols], psum[:, 4 * (g % 2):4 * (g % 2) + 4, 0:DQ], k_h[:, :, cols]).then_inc(k_ready, 1)

            for n in range(4):
                cut(n)
            turn(4)
            for n in range(4, n_before_k):
                if n + 1 < n_before_k:
                    turn(n + 1)
                cut(n)
                if items[n][0] == "g2" and items[n][1] % 2 and items[n][1] >= 3:
                    k_part((items[n][1] - 3) // 2)
            turn(n_before_k)
            k_part(3)
            for n in range(n_before_k, n_before_k + 4):
                if n + 1 < n_before_k + 4:
                    turn(n + 1)
                cut(n)

            def scale_rows(b, nb):
                dve.wait_ge(rstd_ready, 2 * b + nb + 1)
                nc.vector.scalar_tensor_tensor(xrow[nb][:, :], xrow[nb][:, :], rstd[:, nb:nb + 1], norm[:, :],
                                               ALU.mult, ALU.mult).then_inc(row_ready, 1)

            def batch(b, first, last):
                for t in range(4):
                    if t == 2 and not first:
                        scale_rows(b - 1, 1)
                    mb, j, bk = p_tile(t)
                    dve.wait_ge(p_high, 4 * b + t + 1)
                    low(p_cols(p_l, mb, j), bank(bk), p_cols(p_h, mb, j)).then_inc(p_ready, 1)
                for g in range(4):
                    dve.wait_ge(ptl_mm, 4 * b + g + 1)
                    if g >= 2:
                        dve.wait_ge(pt_used, 4 * b + g - 1)
                    nc.vector.tensor_copy(pt_l[:, g % 2].rearrange("p k m -> p (k m)"),
                                          bank(PT_BANKS[g % 2][1])).then_inc(ptl_ready, 1)
                dve.wait_ge(pt_used, 4 * b + 4)
                nc.vector.tensor_reduce(rowmax, psum[:, 2:4, 0:M], AX.X, ALU.max).then_inc(max_done, 1)
                dve.wait_ge(max_done, b + 1)
                nc.vector.tensor_scalar(negmax, rowmax, -SCALE, None, ALU.mult).then_inc(negmax_done, 1)
                if first:
                    turn(pos["g1", 4])
                    for i in range(4, 8):
                        if i < 7:
                            turn(pos["g1", i + 1])
                        cut(pos["g1", i])
                dve.wait_ge(exp_done, 2 * b + 2)
                nc.vector.reciprocal(rowinv, rowsum).then_inc(inv_done, 1)
                dve.wait_ge(inv_done, b + 1)
                for nb in range(NB):
                    nc.vector.tensor_scalar(prob[:, nb, :], prob[:, nb, :], rowinv[:, nb:nb + 1], None,
                                            ALU.mult).then_inc(prob_ready, 1)
                dve.wait_ge(cn_high, b + 1)
                low(ctt_l[:, :, :].rearrange("p j (m c) -> p j m c", m=MB),
                    stage[:, :].rearrange("p (m j c) -> p j m c", m=MB, j=KE),
                    ctt_h[:, :, :].rearrange("p j (m c) -> p j m c", m=MB)).then_inc(cn_ready, 1)
                dve.wait_ge(at_high, b + 1)
                low(at_l[:, :, :].rearrange("p m n -> p (m n)"), bank(4),
                    at_h[:, :, :].rearrange("p m n -> p (m n)")).then_inc(at_ready, 1)

                def turn_x(nb):
                    dve.wait_ge(xs_in, DMA * QUADS * (2 * b + nb + 1))
                    src, dst = turn_views(stage, turned, 4)
                    nc.vector.transpose(dst, src).then_inc(xs_moved, 1)

                if not last:
                    if first:
                        dve.wait_ge(item_ready, len(items))
                    else:
                        dve.wait_ge(ct_ready, b)
                    turn_x(0)
                for i in range(2):
                    dve.wait_ge(tt_high, 2 * b + i + 1)
                    rows = slice(2 * i, 2 * i + 2)
                    low(ctt_l[:, rows, :].rearrange("p j n -> p (j n)"), bank(6 + i),
                        ctt_h[:, rows, :].rearrange("p j n -> p (j n)")).then_inc(tt_ready, 1)
                if not last:
                    for nb in range(NB):
                        if nb == 1:
                            dve.wait_ge(xt_ready, 2 * b + 1)
                            turn_x(1)
                        dve.wait_ge(xt_high, 2 * b + nb + 1)
                        cols = slice(PART * nb, PART * nb + PART)
                        low(xt_l[:, :, cols], turned[:, :].rearrange("p (k n) -> p k n", k=KD),
                            xt_h[:, :, cols]).then_inc(xt_ready, 1)
                    dve.wait_ge(xt_ready, 2 * b + 2)
                    dve.wait_ge(cs_in, DMA * QUADS * (b + 1))
                    src, dst = turn_views(stage, turned, 8)
                    nc.vector.transpose(dst, src).then_inc(cs_moved, 1)
                    dve.wait_ge(ct_high, b + 1)
                    low(ct_l[:, :, :], turned[:, :].rearrange("p (k n) -> p k n", k=KE),
                        ct_h[:, :, :]).then_inc(ct_ready, 1)
                for nb in range(NB):
                    done = 2 * b + nb + 1
                    dve.wait_ge(gate_mm, done)
                    if first and nb == 0:
                        dve.wait_ge(consts_in, 2 * DMA)
                    nc.vector.tensor_tensor(gate[:, :], psum[:, 2 * nb:2 * nb + 2, :].rearrange("p h c -> p (h c)"),
                                            bias[:, :], ALU.add).then_inc(z_ready, 1)
                    dve.wait_ge(tanh_done, done)
                    nc.vector.scalar_tensor_tensor(
                        gate[:, :], gate[:, :], 1.0, psum[:, 4 + 2 * nb:6 + 2 * nb, :].rearrange("p h c -> p (h c)"),
                        ALU.add, ALU.mult).then_inc(gm_ready, 1)
                    dve.wait_ge(gm_ready, done)
                    dve.wait_ge(xrow_in[nb], DMA * (b + 1))
                    nc.vector.scalar_tensor_tensor(xrow[nb][:, :], gate[:, :], 0.5, xrow[nb][:, :],
                                                   ALU.mult, ALU.add).then_inc(f_ready, 1)
                    if nb == 0:
                        scale_rows(b, 0)

            batch(0, True, False)
            with dve.Fori(1, B - 1) as b:
                batch(b, False, False)
            batch(B - 1, False, True)
            scale_rows(B - 1, 1)

        @block.tensor
        def _(pe):
            def product(dst, pairs, start=True, stop=True, **kw):
                n = len(pairs)
                for i, ((ah, al), (mh, ml)) in enumerate(pairs):
                    nc.tensor.matmul(dst, ah, mh, start=start and i == 0, stop=False, **kw)
                    nc.tensor.matmul(dst, ah, ml, start=False, stop=False, **kw)
                    last = nc.tensor.matmul(dst, al, mh, start=False, stop=stop and i == n - 1, **kw)
                return last

            for g in range(4):
                if g >= 2:
                    pe.wait_ge(k_ready, g - 1)
                for h in range(2):
                    for n in range(4):
                        if g == 0 and n % 2 == 0:
                            pe.wait_ge(item_ready, pos["wn", (4 * h + n) // 2] + 1)
                        if n == 0:
                            pe.wait_ge(item_ready, pos["g2", 2 * g + h] + 1)
                        kd = 4 * h + n
                        for e in range(KE):
                            cols = slice(PART * e, PART * e + PART)
                            last = product(psum[:, 4 * (g % 2) + e, 0:DQ],
                                           [((wn_h[:, kd, cols], wn_l[:, kd, cols]),
                                             (g2_h[:, h, n, :], g2_l[:, h, n, :]))],
                                           start=kd == 0, stop=kd == KD - 1)
                    last.then_inc(g2_used, 1)

            def batch(b, first):
                if first:
                    pe.wait_ge(item_ready, pos["ct", 0] + 1)
                else:
                    pe.wait_ge(ct_ready, b)
                for t in range(4):
                    mb, j, bk = p_tile(t)
                    if first:
                        pe.wait_ge(k_ready, 3 if t < 2 else 4)
                    elif t == 0:
                        pe.wait_ge(z_ready, 2 * b - 1)
                    elif t == 2:
                        pe.wait_ge(gm_ready, 2 * b - 1)
                    rows = slice(PART * mb, PART * mb + PART)
                    cols = slice(BANK * j, BANK * j + BANK)
                    product(bank(bk), [((ct_h[:, k, rows], ct_l[:, k, rows]), (wt_h[:, k, cols], wt_l[:, k, cols]))
                                       for k in range(KE)]).then_inc(p_mm, 1)

                def turn_p(g):
                    if g == 0 and not first:
                        pe.wait_ge(gm_ready, 2 * b)
                    if g % 2 == 0:
                        pe.wait_ge(p_ready, 4 * b + g + 2)
                    for part, bk, done in ((p_h, PT_BANKS[g % 2][0], pth_mm), (p_l, PT_BANKS[g % 2][1], ptl_mm)):
                        for kk in range(2):
                            for mb in range(MB):
                                col = PART * (2 * g + kk)
                                last = nc.tensor.matmul(
                                    bank(bk)[:, M * kk + PART * mb:M * kk + PART * mb + PART],
                                    part[:, mb, col:col + PART], ident_r[:, :], start=True, stop=True)
                        last.then_inc(done, 1)

                def scores(g):
                    pe.wait_ge(pth_ready, 4 * b + g + 1)
                    pe.wait_ge(ptl_ready, 4 * b + g + 1)
                    if g == 0:
                        if first:
                            pe.wait_ge(item_ready, pos["xt", 1] + 1)
                        else:
                            pe.wait_ge(xt_ready, 2 * b)
                            pe.wait_ge(z_ready, 2 * b)
                    for kk in range(2):
                        for nb in range(NB):
                            rows = slice(PART * nb, PART * nb + PART)
                            k = 2 * g + kk
                            last = product(psum[:, 2 + nb, 0:M],
                                           [((xt_h[:, k, rows], xt_l[:, k, rows]),
                                             (pt_h[:, g % 2, kk, :], pt_l[:, g % 2, kk, :]))],
                                           start=k == 0, stop=k == KD - 1)
                    last.then_inc(pt_used, 1)

                if first:
                    pe.wait_ge(ident_r_done, 1)
                turn_p(0)
                turn_p(1)
                scores(0)
                turn_p(2)
                scores(1)
                turn_p(3)
                scores(2)
                scores(3)

                def gate_x(nb):
                    rows = slice(PART * nb, PART * nb + PART)
                    for half in range(HALVES):
                        if first and nb == 0:
                            pe.wait_ge(item_ready, pos["g1", 4 * half + 3] + 1)
                        cols = slice(BANK * half, BANK * half + BANK)
                        last = product(bank(2 * nb + half),
                                       [((xt_h[:, k, rows], xt_l[:, k, rows]), (g1_h[:, k, cols], g1_l[:, k, cols]))
                                        for k in range(KD)], stop=False)
                    return last

                gate_x(0)
                pe.wait_ge(prob_ready, 2 * b + 2)
                if first:
                    pe.wait_ge(ident_done, 4)
                for mb in range(MB):
                    for nb in range(NB):
                        last = nc.tensor.transpose(bank(4)[:, N * mb + PART * nb:N * mb + PART * nb + PART],
                                                   prob[:, nb, PART * mb:PART * mb + PART], ident[:, :])
                last.then_inc(at_mm, 1)
                gate_x(1).then_inc(xt_used, 1)

                pe.wait_ge(cn_ready, b + 1)
                pe.wait_ge(at_ready, b + 1)
                for j in range(KE):
                    last = product(bank(6 + j // 2)[:, N * (j % 2):N * (j % 2) + N],
                                   [((ctt_h[:, j, PART * mb:PART * mb + PART], ctt_l[:, j, PART * mb:PART * mb + PART]),
                                     (at_h[:, mb, :], at_l[:, mb, :])) for mb in range(MB)])
                    if j % 2:
                        last.then_inc(tt_mm, 1)

                for nb in range(NB):
                    rows = slice(PART * nb, PART * nb + PART)
                    if nb == 1:
                        pe.wait_ge(tt_ready, 2 * b + 2)
                    for half in range(HALVES):
                        last = product(bank(4 + 2 * nb + half),
                                       [((at_h[:, mb, rows], at_l[:, mb, rows]),
                                         (p_natural(p_h, mb, half), p_natural(p_l, mb, half)))
                                        for mb in range(MB)])
                last.then_inc(m_mm, 1)

                for nb in range(NB):
                    rows = slice(PART * nb, PART * nb + PART)
                    for half in range(HALVES):
                        cols = slice(BANK * half, BANK * half + BANK)
                        last = product(bank(2 * nb + half),
                                       [((ctt_h[:, j, rows], ctt_l[:, j, rows]), (k_h[:, j, cols], k_l[:, j, cols]))
                                        for j in range(KE)], start=False)
                    last.then_inc(gate_mm, 1)

            batch(0, True)
            with pe.Fori(1, B) as b:
                batch(b, False)


_INS = ["x", "ctx_1024", "L0_xattn_W_mem", "L0_xattn_W_gate", "L0_xattn_b_gate", "L0_xattn_norm_w"]


def kernel(**inputs):
    import concourse.bacc as bacc
    import numpy as np
    from concourse.bass_utils import run_bass_kernel_spmd

    nc = bacc.Bacc("TRN2", target_bir_lowering=False, num_devices=1)
    arrays, args = {}, []
    for name in _INS:
        a = np.ascontiguousarray(inputs[name])
        arrays[f"in_{name}"] = a
        args.append(nc.dram_tensor(f"in_{name}", a.shape, mybir.dt.from_np(a.dtype), kind="ExternalInput").ap())
    args.append(nc.dram_tensor("out_0", inputs["x"].shape, F32, kind="ExternalOutput").ap())
    build(nc, *args)
    result = run_bass_kernel_spmd(nc, [arrays], core_ids=[0])
    return result.results[0]["out_0"]
```

```python
from contextlib import ExitStack

import concourse.bass as bass
from concourse import mybir

F32 = mybir.dt.float32
F32R = mybir.dt.float32r
ACT = mybir.ActivationFunctionType
ALU = mybir.AluOpType
AX = mybir.AxisListType

PART = 128
BLK = 32
QUADS = PART // BLK
BANK = 512
EPS = 1e-6


def build(nc, x, ctx_in, w_mem, w_gate, b_gate, norm_w, out):
    B, N, D = x.shape
    M, E = ctx_in.shape[1:]
    NB, MB = N // PART, M // PART
    KD, KE = D // PART, E // PART
    HALVES = D // BANK
    DQ, EQ = D // QUADS, E // QUADS
    SCALE = 1.0 / float(D) ** 0.5
    DMA = 16

    with ExitStack() as ctx:
        def sem(name):
            return ctx.enter_context(nc.semaphore(name))

        def const(name, shape, dtype):
            return ctx.enter_context(nc.sbuf_tensor(name, shape, dtype))

        wt_h, wt_l = (const(f"wt_{s}", [PART, KE, D], F32R) for s in "hl")
        k_h, k_l = (const(f"k_{s}", [PART, KE, D], F32R) for s in "hl")
        g1_h = const("g1_h", [PART, KD, D], F32R)
        g1_l_mem = const("g1_l_mem", [PART, KD * D], F32)
        bias = const("bias", [PART, D], F32)
        norm_mem = const("norm_mem", [PART, D], F32)
        ident = const("ident", [PART, PART], F32)
        stat = const("stat", [PART, 32], F32)
        KB = 1024
        work = const("work", [PART, 68 * KB // 4], F32)

        def at(name, shape, dtype, mem, kb):
            return nc.alloc_sbuf_tensor_at(name, shape, dtype, offset=nc.lookup_mloc(mem).addr + kb * KB)

        norm = at("norm", [PART, D], F32, norm_mem, 0)
        g1_l = at("g1_l", [PART, KD, D], F32R, g1_l_mem, 0)
        wn_h = at("wn_h", [PART, KD, E], F32R, g1_l_mem, 0)
        wn_l = at("wn_l", [PART, KD, E], F32R, g1_l_mem, 16)
        xt_h = at("xt_h", [PART, KD, N], F32R, work, 0)
        xt_l = at("xt_l", [PART, KD, N], F32R, work, 8)
        p_h = at("p_h", [PART, MB, D], F32R, work, 16)
        p_l = at("p_l", [PART, MB, D], F32R, work, 24)
        g2_h = at("g2_h", [PART, 2, 4, DQ], F32R, work, 16)
        g2_l = at("g2_l", [PART, 2, 4, DQ], F32R, work, 24)
        ct_h = at("ct_h", [PART, KE, M], F32R, work, 32)
        ct_l = at("ct_l", [PART, KE, M], F32R, work, 36)
        pt_h = at("pt_h", [PART, 2, 2, M], F32R, work, 32)
        pt_l = at("pt_l", [PART, 2, 2, M], F32R, work, 36)
        prob = at("prob", [PART, NB, M], F32, work, 32)
        at_h = at("at_h", [PART, MB, N], F32R, work, 34)
        at_l = at("at_l", [PART, MB, N], F32R, work, 36)
        p32 = at("p32", [PART, MB, D], F32, work, 40)
        ctt_h = at("ctt_h", [PART, KE, MB * PART], F32R, work, 40)
        ctt_l = at("ctt_l", [PART, KE, MB * PART], F32R, work, 44)
        xrow = [at(f"xrow{i}", [PART, D], F32, work, 48 + 4 * i) for i in range(NB)]
        gate = at("gate", [PART, D], F32, work, 56)
        stage = at("stage", [PART, D], F32, work, 60)
        turned = at("turned", [PART, D], F32, work, 64)
        ring = [stage] + [at(f"ring{i}", [PART, D], F32, work, 48 + 4 * (i - 1)) for i in range(1, 4)]
        turned2 = [turned, at("turned_b", [PART, D], F32, norm_mem, 0)]

        negmax, rowmax = stat[:, 0:NB], stat[:, 2:2 + NB]
        rowsum, rowinv = stat[:, 4:4 + NB], stat[:, 6:6 + NB]
        meansq, guarded, rstd = stat[:, 8:8 + NB], stat[:, 10:10 + NB], stat[:, 12:12 + NB]
        minus_half, eps = stat[:, 14:15], stat[:, 15:16]

        psum = ctx.enter_context(nc.psum_tensor("psum", [PART, 8, BANK], F32))

        def bank(i):
            return psum[:, i, :]

        ring_in = [sem(f"ring{i}_in") for i in range(4)]
        consts_in = sem("consts_in")
        xs_in, cs_in, cn_in = sem("xs_in"), sem("cs_in"), sem("cn_in")
        xrow_in = [sem(f"xrow{i}_in") for i in range(NB)]
        out_done = [sem(f"out{i}_done") for i in range(NB)]
        ident_done = sem("ident_done")
        item_turned = sem("item_turned")
        item_h = sem("item_h")
        item_ready = sem("item_ready")
        k_high, k_ready = sem("k_high"), sem("k_ready")
        g2_used = sem("g2_used")
        xs_moved, cs_moved = sem("xs_moved"), sem("cs_moved")
        xt_high, xt_ready, xt_used = sem("xt_high"), sem("xt_ready"), sem("xt_used")
        ct_high, ct_ready = sem("ct_high"), sem("ct_ready")
        cn_high, cn_ready = sem("cn_high"), sem("cn_ready")
        p_mm, p_even, p_odd = sem("p_mm"), sem("p_even"), sem("p_odd")
        p_high, p_ready = sem("p_high"), sem("p_ready")
        pt_mm, pt_high, pt_ready, pt_used = sem("pt_mm"), sem("pt_high"), sem("pt_ready"), sem("pt_used")
        max_done, negmax_done = sem("max_done"), sem("negmax_done")
        exp_done, inv_done, prob_ready = sem("exp_done"), sem("inv_done"), sem("prob_ready")
        at_mm, at_high, at_ready = sem("at_mm"), sem("at_high"), sem("at_ready")
        tt_mm, tt_high, tt_ready = sem("tt_mm"), sem("tt_high"), sem("tt_ready")
        m_mm, gate_mm = sem("m_mm"), sem("gate_mm")
        z_ready, tanh_done, gm_ready, f_ready = sem("z_ready"), sem("tanh_done"), sem("gm_ready"), sem("f_ready")
        sq_done, guarded_done, rstd_ready, row_ready = (sem("sq_done"), sem("guarded_done"), sem("rstd_ready"),
                                                       sem("row_ready"))

        items = [("g2", 0), ("wn", 0), ("wn", 1), ("wn", 2), ("g2", 1), ("wn", 3)]
        for i in range(4):
            items += [("wt", i), ("g2", i + 2)]
        items += [("ct", 0), ("g2", 6), ("xt", 0), ("g2", 7), ("xt", 1)]
        n_before_k = len(items)
        items += [("g1", i) for i in range(8)]
        pos = {item: n for n, item in enumerate(items)}
        K_PARTS = {("g2", 2 * g + 3): g for g in range(3)}

        def turned_count(n):
            return sum(kind != "wn" for kind, _ in items[:n + 1])

        def ring_count(n):
            return DMA * QUADS * (n // 4 + 1)

        def blocks(mat, rows0, n_rows, col0, n_cols):
            return mat[rows0:rows0 + n_rows, col0:col0 + n_cols].rearrange("(i c) f -> c i f", c=BLK)

        def on_stage(stage_buf, q, i_count):
            return stage_buf[BLK * q:BLK * q + BLK, :].rearrange("c (i f) -> c i f", i=i_count)

        def load_item(sp, n):
            kind, i = items[n]
            buf, done = ring[n % 4], ring_in[n % 4]
            for q in range(QUADS):
                if kind == "wn":
                    r0 = DQ * q + BLK * 2 * i
                    sp.dma_start(buf[BLK * q:BLK * q + BLK, :].rearrange("r (k e) -> r k e", k=2),
                                 w_mem[r0:r0 + 2 * BLK, :].rearrange("(k r) e -> r k e", k=2)).then_inc(done, DMA)
                elif kind in ("g1", "g2"):
                    g, h = g_piece(kind, i)
                    col = (D if kind == "g2" else 0) + DQ * q + PART * h
                    sp.dma_start(on_stage(buf, q, 8), blocks(w_gate, 256 * g, 256, col, PART)).then_inc(done, DMA)
                elif kind == "wt":
                    sp.dma_start(on_stage(buf, q, 8), blocks(w_mem, 256 * i, 256, EQ * q, EQ)).then_inc(done, DMA)
                elif kind == "ct":
                    sp.dma_start(on_stage(buf, q, 8), blocks(ctx_in[0], 0, M, EQ * q, EQ)).then_inc(done, DMA)
                else:
                    sp.dma_start(on_stage(buf, q, 4),
                                 blocks(x[0], PART * i, PART, DQ * q, DQ)).then_inc(done, DMA)

        def g_piece(kind, i):
            return (i // 2, i % 2) if kind == "g2" else (i % 4, i // 4)

        def turn_views(src, dst, i_count):
            k = D // (i_count * BLK)
            return (src[:, :].rearrange("p (i k r) -> p k i r", i=i_count, k=k),
                    dst[:, :].rearrange("p (k i c) -> p k i c", k=k, i=i_count))

        def item_parts(n):
            kind, i = items[n]
            src = turned2[n % 2]
            if kind == "wn":
                return (ring[n % 4][:, :].rearrange("p (k e) -> p k e", k=2),
                        wn_h[:, 2 * i:2 * i + 2, :], wn_l[:, 2 * i:2 * i + 2, :])
            if kind == "xt":
                v = src[:, :].rearrange("p (k n) -> p k n", k=KD)
                return v, xt_h[:, :, PART * i:PART * i + PART], xt_l[:, :, PART * i:PART * i + PART]
            v = src[:, :].rearrange("p (k n) -> p k n", k=4)
            if kind == "g2":
                return v, g2_h[:, i % 2], g2_l[:, i % 2]
            if kind == "wt":
                return (src[:, :].rearrange("p (e k r) -> p e k r", e=KE, k=KD),
                        *(w[:, :, :].rearrange("p e (k q r) -> p e k q r", k=KD, q=QUADS)[:, :, :, i, :]
                          for w in (wt_h, wt_l)))
            if kind == "ct":
                return v, ct_h[:, :, :], ct_l[:, :, :]
            g, h = g_piece(kind, i)
            return (v, g1_h[:, 4 * h:4 * h + 4, 256 * g:256 * g + 256],
                    g1_l[:, 4 * h:4 * h + 4, 256 * g:256 * g + 256])

        def p_tile(t):
            return t // 2, t % 2, (0, 1, 4, 5)[t]

        def p_cols(buf, mb, j):
            return buf[:, mb, BANK * j:BANK * j + BANK]

        def p_natural(buf, mb, half):
            return buf[:, mb, :].rearrange("p (k q r) -> p q k r", k=KD, q=QUADS)[:, 2 * half:2 * half + 2]

        PT_BANKS = (6, 7, 4, 5)
        block = ctx.enter_context(nc.Block())

        @block.sync
        def _(sp):
            for n in range(4):
                load_item(sp, n)
            sp.dma_start(bias[:, :], b_gate.rearrange("(a d) -> a d", a=1).to_broadcast((PART, D))
                         ).then_inc(consts_in, DMA)
            for n in range(4, len(items)):
                if items[n - 4][0] == "wn":
                    sp.wait_ge(item_ready, n - 3)
                else:
                    sp.wait_ge(item_turned, turned_count(n - 4))
                load_item(sp, n)

            def load_c_rows(b, first):
                if first:
                    sp.wait_ge(item_turned, turned_count(24))
                else:
                    sp.wait_ge(cs_moved, b)
                sp.dma_start(stage[:, :].rearrange("p (m e) -> p m e", m=MB),
                             ctx_in[bass.ds(b, 1)].rearrange("a (m p) e -> p (a m) e", p=PART)).then_inc(cn_in, DMA)

            def load_x_rows(b, first):
                for nb in range(NB):
                    if first:
                        sp.wait_ge(item_turned, turned_count(len(items) - 1))
                    else:
                        sp.wait_ge(out_done[nb], DMA * b)
                    sp.dma_start(xrow[nb][:, :],
                                 x[bass.ds(b, 1), PART * nb:PART * nb + PART, :].rearrange("a p d -> p (a d)")
                                 ).then_inc(xrow_in[nb], DMA)

            def store_rows(b):
                for nb in range(NB):
                    sp.wait_ge(row_ready, 2 * b + nb + 1)
                    sp.dma_start(out[bass.ds(b, 1), PART * nb:PART * nb + PART, :].rearrange("a p d -> p (a d)"),
                                 xrow[nb][:, :]).then_inc(out_done[nb], DMA)

            sp.wait_ge(item_ready, len(items))
            sp.dma_start(norm[:, :], norm_w.rearrange("(a d) -> a d", a=1).to_broadcast((PART, D))
                         ).then_inc(consts_in, DMA)
            load_c_rows(0, True)
            load_x_rows(0, True)
            with sp.Fori(1, B) as b:
                for nb in range(NB):
                    if nb == 0:
                        sp.wait_ge(cn_ready, b)
                    else:
                        sp.wait_ge(xs_moved, 2 * b - 1)
                    for q in range(QUADS):
                        sp.dma_start(on_stage(stage, q, 4),
                                     x[bass.ds(b, 1), PART * nb:PART * nb + PART, DQ * q:DQ * q + DQ].rearrange(
                                         "a (i c) f -> c (a i) f", c=BLK)).then_inc(xs_in, DMA)
                sp.wait_ge(xs_moved, 2 * b)
                for q in range(QUADS):
                    sp.dma_start(on_stage(stage, q, 8),
                                 ctx_in[bass.ds(b, 1), :, EQ * q:EQ * q + EQ].rearrange(
                                     "a (i c) f -> c (a i) f", c=BLK)).then_inc(cs_in, DMA)
                load_c_rows(b, False)
                store_rows(b - 1)
                load_x_rows(b, False)
            store_rows(B - 1)
            for nb in range(NB):
                sp.wait_ge(out_done[nb], DMA * B)

        @block.gpsimd
        def _(pool):
            pool.memset(ident[:, :], 0.0).then_inc(ident_done, 1)
            pool.memset(minus_half, -0.5).then_inc(ident_done, 1)
            pool.memset(eps, EPS).then_inc(ident_done, 1)
            pool.wait_ge(ident_done, 3)
            pool.affine_select(out=ident[:, :], in_=ident[:, :], compare_op=ALU.not_equal, fill=1.0, base=0,
                               pattern=[[-1, PART]], channel_multiplier=1).then_inc(ident_done, 1)

            def batch(b):
                for nb in range(NB):
                    done = 2 * b + nb + 1
                    pool.wait_ge(sq_done, done)
                    pool.tensor_tensor(guarded[:, nb:nb + 1], meansq[:, nb:nb + 1], eps,
                                       ALU.add).then_inc(guarded_done, 1)
                    pool.wait_ge(guarded_done, done)
                    pool.tensor_tensor(rstd[:, nb:nb + 1], guarded[:, nb:nb + 1], minus_half,
                                       ALU.pow).then_inc(rstd_ready, 1)

            batch(0)
            with pool.Fori(1, B) as b:
                batch(b)

        @block.scalar
        def _(act):
            def copy(dst, src):
                return nc.scalar.activation(dst, src, ACT.Copy)

            def item(n):
                kind, i = items[n]
                src, high, _ = item_parts(n)
                if kind == "wn":
                    act.wait_ge(ring_in[n % 4], ring_count(n))
                else:
                    act.wait_ge(item_turned, turned_count(n))
                if kind == "g2" and i >= 2:
                    act.wait_ge(g2_used, i - 1)
                copy(high, src).then_inc(item_h, 1)

            def k_part(g):
                act.wait_ge(g2_used, 2 * g + 2)
                copy(k_h[:, :, DQ * g:DQ * g + DQ],
                     psum[:, 4 * (g % 2):4 * (g % 2) + 4, 0:DQ]).then_inc(k_high, 1)

            for n in range(n_before_k):
                item(n)
                if items[n] in K_PARTS:
                    k_part(K_PARTS[items[n]])
            k_part(3)
            for i in range(4):
                item(pos["g1", i])

            def batch(b, first, last):
                for t in (0, 2):
                    mb, j, bk = p_tile(t)
                    act.wait_ge(p_mm, 4 * b + t + 1)
                    copy(p_cols(p32, mb, j), bank(bk)).then_inc(p_even, 1)
                if first:
                    for i in range(4, 8):
                        item(pos["g1", i])
                for g in range(4):
                    act.wait_ge(pt_mm, 4 * b + g + 1)
                    if g >= 2:
                        act.wait_ge(pt_used, 4 * b + g - 1)
                    copy(pt_h[:, g % 2].rearrange("p k m -> p (k m)"), bank(PT_BANKS[g])).then_inc(pt_high, 1)
                act.wait_ge(negmax_done, b + 1)
                for nb in range(NB):
                    nc.scalar.activation(prob[:, nb, :], psum[:, 2 + nb, 0:M], ACT.Exp, bias=negmax[:, nb:nb + 1],
                                         scale=SCALE, accum_out=rowsum[:, nb:nb + 1]).then_inc(exp_done, 1)
                for mb in range(MB):
                    copy(p_h[:, mb, :], p32[:, mb, :]).then_inc(p_high, 1)
                act.wait_ge(p_ready, 2 * b + 2)
                act.wait_ge(cn_in, DMA * (b + 1))
                copy(ctt_h[:, :, :].rearrange("p j (m c) -> p j m c", m=MB),
                     stage[:, :].rearrange("p (m j c) -> p j m c", m=MB, j=KE)).then_inc(cn_high, 1)
                act.wait_ge(at_mm, b + 1)
                copy(at_h[:, :, :].rearrange("p m n -> p (m n)"), bank(4)).then_inc(at_high, 1)
                for i in range(2):
                    act.wait_ge(tt_mm, 2 * b + i + 1)
                    copy(ctt_h[:, 2 * i:2 * i + 2, :].rearrange("p j n -> p (j n)"),
                         bank(6 + i)).then_inc(tt_high, 1)
                if not last:
                    act.wait_ge(xt_used, b + 1)
                    for nb in range(NB):
                        act.wait_ge(xs_moved, 2 * b + nb + 1)
                        copy(xt_h[:, :, PART * nb:PART * nb + PART],
                             turned[:, :].rearrange("p (k n) -> p k n", k=KD)).then_inc(xt_high, 1)
                    act.wait_ge(cs_moved, b + 1)
                    act.wait_ge(m_mm, b + 1)
                    copy(ct_h[:, :, :], turned[:, :].rearrange("p (k n) -> p k n", k=KE)).then_inc(ct_high, 1)
                for nb in range(NB):
                    done = 2 * b + nb + 1
                    act.wait_ge(z_ready, done)
                    nc.scalar.activation(gate[:, :], gate[:, :], ACT.Tanh, scale=0.5).then_inc(tanh_done, 1)
                    act.wait_ge(f_ready, done)
                    nc.scalar.activation(turned[:, :], xrow[nb][:, :], ACT.Square, scale=SCALE,
                                         accum_out=meansq[:, nb:nb + 1]).then_inc(sq_done, 1)

            batch(0, True, False)
            with act.Fori(1, B - 1) as b:
                batch(b, False, False)
            batch(B - 1, False, True)

        @block.vector
        def _(dve):
            def low(dst, src, high):
                return nc.vector.tensor_tensor(dst, src, high.bitcast(F32), ALU.subtract)

            def turn(n):
                kind, i = items[n]
                dve.wait_ge(ring_in[n % 4], ring_count(n))
                if n >= 2:
                    dve.wait_ge(item_ready, n - 1)
                src, dst = turn_views(ring[n % 4], turned2[n % 2], 4 if kind == "xt" else 8)
                nc.vector.transpose(dst, src).then_inc(item_turned, 1)

            def cut(n):
                kind, i = items[n]
                src, high, lo = item_parts(n)
                dve.wait_ge(item_h, n + 1)
                if kind == "g1":
                    dve.wait_ge(g2_used, 8)
                low(lo, src, high).then_inc(item_ready, 1)

            def k_part(g):
                dve.wait_ge(k_high, g + 1)
                cols = slice(DQ * g, DQ * g + DQ)
                low(k_l[:, :, cols], psum[:, 4 * (g % 2):4 * (g % 2) + 4, 0:DQ], k_h[:, :, cols]).then_inc(k_ready, 1)

            turn(0)
            for n in range(n_before_k):
                if n + 1 < n_before_k and items[n + 1][0] != "wn":
                    turn(n + 1)
                cut(n)
                if items[n] in K_PARTS:
                    k_part(K_PARTS[items[n]])
            turn(n_before_k)
            k_part(3)
            for n in range(n_before_k, n_before_k + 4):
                if n + 1 < n_before_k + 4:
                    turn(n + 1)
                cut(n)

            def scale_rows(b, nb):
                dve.wait_ge(rstd_ready, 2 * b + nb + 1)
                nc.vector.scalar_tensor_tensor(xrow[nb][:, :], xrow[nb][:, :], rstd[:, nb:nb + 1], norm[:, :],
                                               ALU.mult, ALU.mult).then_inc(row_ready, 1)

            def batch(b, first, last):
                for t in (1, 3):
                    if t == 3 and not first:
                        scale_rows(b - 1, 1)
                    mb, j, bk = p_tile(t)
                    dve.wait_ge(p_mm, 4 * b + t + 1)
                    nc.vector.tensor_copy(p_cols(p32, mb, j), bank(bk)).then_inc(p_odd, 1)
                if first:
                    turn(pos["g1", 4])
                    for i in range(4, 8):
                        if i < 7:
                            turn(pos["g1", i + 1])
                        cut(pos["g1", i])
                for g in range(4):
                    dve.wait_ge(pt_high, 4 * b + g + 1)
                    low(pt_l[:, g % 2].rearrange("p k m -> p (k m)"), bank(PT_BANKS[g]),
                        pt_h[:, g % 2].rearrange("p k m -> p (k m)")).then_inc(pt_ready, 1)
                dve.wait_ge(pt_used, 4 * b + 4)
                nc.vector.tensor_reduce(rowmax, psum[:, 2:4, 0:M], AX.X, ALU.max).then_inc(max_done, 1)
                dve.wait_ge(max_done, b + 1)
                nc.vector.tensor_scalar(negmax, rowmax, -SCALE, None, ALU.mult).then_inc(negmax_done, 1)
                dve.wait_ge(exp_done, 2 * b + 2)
                nc.vector.reciprocal(rowinv, rowsum).then_inc(inv_done, 1)
                dve.wait_ge(inv_done, b + 1)
                for nb in range(NB):
                    nc.vector.tensor_scalar(prob[:, nb, :], prob[:, nb, :], rowinv[:, nb:nb + 1], None,
                                            ALU.mult).then_inc(prob_ready, 1)
                for mb in range(MB):
                    dve.wait_ge(p_high, 2 * b + mb + 1)
                    low(p_l[:, mb, :], p32[:, mb, :], p_h[:, mb, :]).then_inc(p_ready, 1)
                dve.wait_ge(cn_high, b + 1)
                low(ctt_l[:, :, :].rearrange("p j (m c) -> p j m c", m=MB),
                    stage[:, :].rearrange("p (m j c) -> p j m c", m=MB, j=KE),
                    ctt_h[:, :, :].rearrange("p j (m c) -> p j m c", m=MB)).then_inc(cn_ready, 1)
                dve.wait_ge(at_high, b + 1)
                low(at_l[:, :, :].rearrange("p m n -> p (m n)"), bank(4),
                    at_h[:, :, :].rearrange("p m n -> p (m n)")).then_inc(at_ready, 1)

                def turn_x(nb):
                    dve.wait_ge(xs_in, DMA * QUADS * (2 * b + nb + 1))
                    src, dst = turn_views(stage, turned, 4)
                    nc.vector.transpose(dst, src).then_inc(xs_moved, 1)

                if not last:
                    if first:
                        dve.wait_ge(item_ready, len(items))
                    else:
                        dve.wait_ge(ct_ready, b)
                    turn_x(0)
                for i in range(2):
                    dve.wait_ge(tt_high, 2 * b + i + 1)
                    rows = slice(2 * i, 2 * i + 2)
                    low(ctt_l[:, rows, :].rearrange("p j n -> p (j n)"), bank(6 + i),
                        ctt_h[:, rows, :].rearrange("p j n -> p (j n)")).then_inc(tt_ready, 1)
                if not last:
                    for nb in range(NB):
                        if nb == 1:
                            dve.wait_ge(xt_ready, 2 * b + 1)
                            turn_x(1)
                        dve.wait_ge(xt_high, 2 * b + nb + 1)
                        cols = slice(PART * nb, PART * nb + PART)
                        low(xt_l[:, :, cols], turned[:, :].rearrange("p (k n) -> p k n", k=KD),
                            xt_h[:, :, cols]).then_inc(xt_ready, 1)
                    dve.wait_ge(xt_ready, 2 * b + 2)
                    dve.wait_ge(cs_in, DMA * QUADS * (b + 1))
                    src, dst = turn_views(stage, turned, 8)
                    nc.vector.transpose(dst, src).then_inc(cs_moved, 1)
                    dve.wait_ge(ct_high, b + 1)
                    low(ct_l[:, :, :], turned[:, :].rearrange("p (k n) -> p k n", k=KE),
                        ct_h[:, :, :]).then_inc(ct_ready, 1)
                if first:
                    dve.wait_ge(consts_in, 2 * DMA)
                for nb in range(NB):
                    done = 2 * b + nb + 1
                    dve.wait_ge(gate_mm, done)
                    if nb == 1:
                        dve.wait_ge(f_ready, done - 1)
                    nc.vector.tensor_tensor(gate[:, :], psum[:, 2 * nb:2 * nb + 2, :].rearrange("p h c -> p (h c)"),
                                            bias[:, :], ALU.add).then_inc(z_ready, 1)
                    if nb == 1:
                        scale_rows(b, 0)
                    dve.wait_ge(tanh_done, done)
                    nc.vector.scalar_tensor_tensor(
                        gate[:, :], gate[:, :], 1.0, psum[:, 4 + 2 * nb:6 + 2 * nb, :].rearrange("p h c -> p (h c)"),
                        ALU.add, ALU.mult).then_inc(gm_ready, 1)
                    dve.wait_ge(gm_ready, done)
                    dve.wait_ge(xrow_in[nb], DMA * (b + 1))
                    nc.vector.scalar_tensor_tensor(xrow[nb][:, :], gate[:, :], 0.5, xrow[nb][:, :],
                                                   ALU.mult, ALU.add).then_inc(f_ready, 1)

            batch(0, True, False)
            with dve.Fori(1, B - 1) as b:
                batch(b, False, False)
            batch(B - 1, False, True)
            scale_rows(B - 1, 1)

        @block.tensor
        def _(pe):
            def product(tiles, pairs, start=True, stop=True):
                last = [None] * len(tiles)
                for i, ((ah, al), moving) in enumerate(pairs):
                    for tile, (mh, ml) in zip(tiles, moving):
                        nc.tensor.matmul(tile, ah, mh, start=start and i == 0, stop=False)
                        nc.tensor.matmul(tile, ah, ml, start=False, stop=False)
                    for t, (tile, (mh, ml)) in enumerate(zip(tiles, moving)):
                        last[t] = nc.tensor.matmul(tile, al, mh, start=False, stop=stop and i == len(pairs) - 1)
                return last

            HALF = [slice(BANK * half, BANK * half + BANK) for half in range(HALVES)]

            for g in range(4):
                if g >= 2:
                    pe.wait_ge(k_ready, g - 1)
                for h in range(2):
                    for n in range(4):
                        if n == 0:
                            pe.wait_ge(item_ready, pos["g2", 2 * g + h] + 1)
                        if g == 0 and n % 2 == 0:
                            pe.wait_ge(item_ready, pos["wn", (4 * h + n) // 2] + 1)
                        kd = 4 * h + n
                        for e in range(KE):
                            cols = slice(PART * e, PART * e + PART)
                            last = product([psum[:, 4 * (g % 2) + e, 0:DQ]],
                                           [((wn_h[:, kd, cols], wn_l[:, kd, cols]),
                                             [(g2_h[:, h, n, :], g2_l[:, h, n, :])])],
                                           start=kd == 0, stop=kd == KD - 1)
                    last[0].then_inc(g2_used, 1)

            def batch(b, first):
                if first:
                    pe.wait_ge(item_ready, pos["ct", 0] + 1)
                else:
                    pe.wait_ge(ct_ready, b)
                for mb in range(MB):
                    if first:
                        pe.wait_ge(k_ready, 3 + mb)
                    elif mb == 0:
                        pe.wait_ge(z_ready, 2 * b - 1)
                    else:
                        pe.wait_ge(gm_ready, 2 * b - 1)
                    rows = slice(PART * mb, PART * mb + PART)
                    tiles = [bank(p_tile(2 * mb + j)[2]) for j in range(2)]
                    for last in product(tiles, [((ct_h[:, k, rows], ct_l[:, k, rows]),
                                                 [(wt_h[:, k, cols], wt_l[:, k, cols]) for cols in HALF])
                                                for k in range(KE)]):
                        last.then_inc(p_mm, 1)

                def turn_p(g):
                    if g == 0 and not first:
                        pe.wait_ge(gm_ready, 2 * b)
                    if g == 0:
                        pe.wait_ge(p_even, 2 * b + 2)
                    if g == 2:
                        pe.wait_ge(p_odd, 2 * b + 2)
                    for kk in range(2):
                        for mb in range(MB):
                            col = PART * (2 * g + kk)
                            last = nc.tensor.transpose(
                                bank(PT_BANKS[g])[:, M * kk + PART * mb:M * kk + PART * mb + PART],
                                p32[:, mb, col:col + PART], ident[:, :])
                    last.then_inc(pt_mm, 1)

                def scores(g):
                    pe.wait_ge(pt_ready, 4 * b + g + 1)
                    if g == 0:
                        if first:
                            pe.wait_ge(item_ready, pos["xt", 1] + 1)
                        else:
                            pe.wait_ge(z_ready, 2 * b)
                    for kk in range(2):
                        for nb in range(NB):
                            rows = slice(PART * nb, PART * nb + PART)
                            k = 2 * g + kk
                            last = product([psum[:, 2 + nb, 0:M]],
                                           [((xt_h[:, k, rows], xt_l[:, k, rows]),
                                             [(pt_h[:, g % 2, kk, :], pt_l[:, g % 2, kk, :])])],
                                           start=k == 0, stop=k == KD - 1)
                    last[0].then_inc(pt_used, 1)

                def gate_x(nb, k0, k1):
                    rows = slice(PART * nb, PART * nb + PART)
                    return product([bank(2 * nb), bank(2 * nb + 1)],
                                   [((xt_h[:, k, rows], xt_l[:, k, rows]),
                                     [(g1_h[:, k, cols], g1_l[:, k, cols]) for cols in HALF])
                                    for k in range(k0, k1)], start=k0 == 0, stop=False)[-1]

                pe.wait_ge(p_even, 2 * b + 1)
                pe.wait_ge(p_odd, 2 * b + 1)
                if first:
                    pe.wait_ge(item_ready, pos["g1", 3] + 1)
                    pe.wait_ge(ident_done, 4)
                else:
                    pe.wait_ge(xt_ready, 2 * b)
                gate_x(0, 0, 2)
                turn_p(0)
                turn_p(1)
                gate_x(0, 2, 4)
                scores(0)
                turn_p(2)
                scores(1)
                turn_p(3)
                if first:
                    pe.wait_ge(item_ready, pos["g1", 7] + 1)
                gate_x(0, 4, 5)
                scores(2)
                scores(3)
                gate_x(0, 5, KD)
                pe.wait_ge(exp_done, 2 * b + 2)
                gate_x(1, 0, 4)

                pe.wait_ge(prob_ready, 2 * b + 2)
                for mb in range(MB):
                    for nb in range(NB):
                        last = nc.tensor.transpose(bank(4)[:, N * mb + PART * nb:N * mb + PART * nb + PART],
                                                   prob[:, nb, PART * mb:PART * mb + PART], ident[:, :])
                last.then_inc(at_mm, 1)
                gate_x(1, 4, KD).then_inc(xt_used, 1)

                pe.wait_ge(cn_ready, b + 1)
                pe.wait_ge(at_ready, b + 1)
                for j in range(KE):
                    last = product([bank(6 + j // 2)[:, N * (j % 2):N * (j % 2) + N]],
                                   [((ctt_h[:, j, PART * mb:PART * mb + PART], ctt_l[:, j, PART * mb:PART * mb + PART]),
                                     [(at_h[:, mb, :], at_l[:, mb, :])]) for mb in range(MB)])
                    if j % 2:
                        last[0].then_inc(tt_mm, 1)

                pe.wait_ge(p_ready, 2 * b + 2)
                for nb in range(NB):
                    rows = slice(PART * nb, PART * nb + PART)
                    if nb == 1:
                        pe.wait_ge(tt_ready, 2 * b + 2)
                    last = product([bank(4 + 2 * nb), bank(5 + 2 * nb)],
                                   [((at_h[:, mb, rows], at_l[:, mb, rows]),
                                     [(p_natural(p_h, mb, half), p_natural(p_l, mb, half)) for half in range(HALVES)])
                                    for mb in range(MB)])
                last[-1].then_inc(m_mm, 1)

                for nb in range(NB):
                    rows = slice(PART * nb, PART * nb + PART)
                    last = product([bank(2 * nb), bank(2 * nb + 1)],
                                   [((ctt_h[:, j, rows], ctt_l[:, j, rows]),
                                     [(k_h[:, j, cols], k_l[:, j, cols]) for cols in HALF])
                                    for j in range(KE)], start=False)
                    last[-1].then_inc(gate_mm, 1)

            batch(0, True)
            with pe.Fori(1, B) as b:
                batch(b, False)


_INS = ["x", "ctx_1024", "L0_xattn_W_mem", "L0_xattn_W_gate", "L0_xattn_b_gate", "L0_xattn_norm_w"]


def kernel(**inputs):
    import concourse.bacc as bacc
    import numpy as np
    from concourse.bass_utils import run_bass_kernel_spmd

    nc = bacc.Bacc("TRN2", target_bir_lowering=False, num_devices=1)
    arrays, args = {}, []
    for name in _INS:
        a = np.ascontiguousarray(inputs[name])
        arrays[f"in_{name}"] = a
        args.append(nc.dram_tensor(f"in_{name}", a.shape, mybir.dt.from_np(a.dtype), kind="ExternalInput").ap())
    args.append(nc.dram_tensor("out_0", inputs["x"].shape, F32, kind="ExternalOutput").ap())
    build(nc, *args)
    result = run_bass_kernel_spmd(nc, [arrays], core_ids=[0])
    return result.results[0]["out_0"]
```

```python
from contextlib import ExitStack

import concourse.bass as bass
from concourse import mybir

F32 = mybir.dt.float32
F32R = mybir.dt.float32r
ACT = mybir.ActivationFunctionType
ALU = mybir.AluOpType
AX = mybir.AxisListType

PART = 128
BLK = 32
QUADS = PART // BLK
BANK = 512
EPS = 1e-6


def build(nc, x, ctx_in, w_mem, w_gate, b_gate, norm_w, out):
    B, N, D = x.shape
    M, E = ctx_in.shape[1:]
    NB, MB = N // PART, M // PART
    KD, KE = D // PART, E // PART
    HALVES = D // BANK
    DQ, EQ = D // QUADS, E // QUADS
    SCALE = 1.0 / float(D) ** 0.5
    DMA = 16

    with ExitStack() as ctx:
        def sem(name):
            return ctx.enter_context(nc.semaphore(name))

        def const(name, shape, dtype):
            return ctx.enter_context(nc.sbuf_tensor(name, shape, dtype))

        wt_h, wt_l = (const(f"wt_{s}", [PART, KE, D], F32R) for s in "hl")
        k_h, k_l = (const(f"k_{s}", [PART, KE, D], F32R) for s in "hl")
        g1_h = const("g1_h", [PART, KD, D], F32R)
        g1_l_mem = const("g1_l_mem", [PART, KD * D], F32)
        bias = const("bias", [PART, D], F32)
        norm_mem = const("norm_mem", [PART, D], F32)
        stat = const("stat", [PART, 32], F32)
        KB = 1024
        work = const("work", [PART, 68 * KB // 4], F32)

        def at(name, shape, dtype, mem, kb):
            return nc.alloc_sbuf_tensor_at(name, shape, dtype, offset=nc.lookup_mloc(mem).addr + kb * KB)

        norm = at("norm", [PART, D], F32, norm_mem, 0)
        g1_l = at("g1_l", [PART, KD, D], F32R, g1_l_mem, 0)
        wn_h = at("wn_h", [PART, KD, E], F32R, g1_l_mem, 0)
        wn_l = at("wn_l", [PART, KD, E], F32R, g1_l_mem, 16)
        xt_h = at("xt_h", [PART, KD, N], F32R, work, 0)
        xt_l = at("xt_l", [PART, KD, N], F32R, work, 8)
        p_h = at("p_h", [PART, MB, D], F32R, work, 16)
        p_l = at("p_l", [PART, MB, D], F32R, work, 24)
        g2_h = at("g2_h", [PART, 2, 4, DQ], F32R, work, 16)
        g2_l = at("g2_l", [PART, 2, 4, DQ], F32R, work, 24)
        ct_h = at("ct_h", [PART, KE, M], F32R, work, 32)
        ct_l = at("ct_l", [PART, KE, M], F32R, work, 36)
        pt_h = at("pt_h", [PART, KD, M], F32R, work, 32)
        pt_l = at("pt_l", [PART, KD, M], F32R, work, 40)
        pt32 = at("pt32", [PART, KD, M], F32, work, 40)
        prob = at("prob", [PART, NB, M], F32, work, 32)
        at_h = at("at_h", [PART, MB, N], F32R, work, 34)
        at_l = at("at_l", [PART, MB, N], F32R, work, 36)
        at32 = at("at32", [PART, MB, N], F32, work, 36)
        ctt_h = at("ctt_h", [PART, KE, MB * PART], F32R, work, 40)
        ctt_l = at("ctt_l", [PART, KE, MB * PART], F32R, work, 44)
        xrow = [at(f"xrow{i}", [PART, D], F32, work, 48 + 4 * i) for i in range(NB)]
        gate = at("gate", [PART, D], F32, work, 56)
        stage = at("stage", [PART, D], F32, work, 60)
        turned = at("turned", [PART, D], F32, work, 64)
        ring = [stage] + [at(f"ring{i}", [PART, D], F32, work, 48 + 4 * (i - 1)) for i in range(1, 4)]
        turned_bufs = [turned, at("turned_b", [PART, D], F32, norm_mem, 0),
                       at("turned_c", [PART, D], F32, work, 40), at("turned_d", [PART, D], F32, work, 44)]

        negmax, rowmax = stat[:, 0:NB], stat[:, 2:2 + NB]
        rowsum, rowinv = stat[:, 4:4 + NB], stat[:, 6:6 + NB]
        meansq, guarded, rstd = stat[:, 8:8 + NB], stat[:, 10:10 + NB], stat[:, 12:12 + NB]
        minus_half, eps = stat[:, 14:15], stat[:, 15:16]
        half_sq = stat[:, 16:16 + HALVES]

        psum = ctx.enter_context(nc.psum_tensor("psum", [PART, 8, BANK], F32))

        def bank(i):
            return psum[:, i, :]

        ring_in = [sem(f"ring{i}_in") for i in range(4)]
        consts_in = sem("consts_in")
        xs_in = [sem(f"xs{i}_in") for i in range(NB)]
        cs_in, cn_in = sem("cs_in"), sem("cn_in")
        xrow_in = [sem(f"xrow{i}_in") for i in range(NB)]
        out_done = [sem(f"out{i}_done") for i in range(NB)]
        consts_done = sem("consts_done")
        item_turned = sem("item_turned")
        item_h = sem("item_h")
        item_low = sem("item_low")
        item_low_pool = sem("item_low_pool")
        k_high, k_ready = sem("k_high"), sem("k_ready")
        g2_used = sem("g2_used")
        half_turned, half_h, half_low = sem("half_turned"), sem("half_h"), sem("half_low")
        xs_moved, cs_moved = sem("xs_moved"), sem("cs_moved")
        xt_high, xt_ready, xt_used = sem("xt_high"), sem("xt_ready"), sem("xt_used")
        ct_high, ct_ready = sem("ct_high"), sem("ct_ready")
        cn_high, cn_ready = sem("cn_high"), sem("cn_ready")
        p_mm, p_high, p_ready = sem("p_mm"), sem("p_high"), sem("p_ready")
        p_turned = sem("p_turned")
        pt_high, pt_ready = sem("pt_high"), sem("pt_ready")
        s_mm = sem("s_mm")
        max_done, negmax_done = sem("max_done"), sem("negmax_done")
        exp_done, inv_done, prob_ready = sem("exp_done"), sem("inv_done"), sem("prob_ready")
        at_turned, at_high, at_ready = sem("at_turned"), sem("at_high"), sem("at_ready")
        tt_mm, tt_high, tt_ready = sem("tt_mm"), sem("tt_high"), sem("tt_ready")
        m_mm, gate_mm = sem("m_mm"), sem("gate_mm")
        z_ready, tanh_done, gm_ready, f_ready = sem("z_ready"), sem("tanh_done"), sem("gm_ready"), sem("f_ready")
        sq_done, guarded_done, rstd_ready, row_ready = (sem("sq_done"), sem("guarded_done"), sem("rstd_ready"),
                                                       sem("row_ready"))

        items = [("g2", 0), ("wn", 0), ("wn", 1), ("g2", 1), ("wn", 2), ("wn", 3)]
        for i in range(4):
            items += [("g2", i + 2), ("wt", i)]
        items += [("ct", 0), ("g2", 6), ("xt", 0), ("g2", 7), ("xt", 1)]
        n_before_k = len(items)
        items += [("g1", i) for i in range(8)]
        pos = {item: n for n, item in enumerate(items)}
        K_PARTS = {("g2", 2 * g + 3): g for g in range(3)}

        def turned_count(n):
            return sum(kind != "wn" for kind, _ in items[:n + 1])

        POOL_ITEMS = {("wn", i) for i in (2, 3)} | {("wt", i) for i in range(4)} | {("g1", i) for i in (1, 3, 4, 5)}

        def is_cut(n):
            by_pool = items[n] in POOL_ITEMS
            count = sum((item in POOL_ITEMS) == by_pool for item in items[:n + 1])
            return (item_low_pool if by_pool else item_low), count

        def turned_buf(n):
            return turned_count(n) % 4

        def ring_count(n):
            return DMA * QUADS * (n // 4 + 1)

        def blocks(mat, rows0, n_rows, col0, n_cols):
            return mat[rows0:rows0 + n_rows, col0:col0 + n_cols].rearrange("(i c) f -> c i f", c=BLK)

        def on_stage(stage_buf, q, i_count):
            return stage_buf[BLK * q:BLK * q + BLK, :].rearrange("c (i f) -> c i f", i=i_count)

        def load_item(sp, n):
            kind, i = items[n]
            buf, done = ring[n % 4], ring_in[n % 4]
            for q in range(QUADS):
                if kind == "wn":
                    r0 = DQ * q + BLK * 2 * i
                    sp.dma_start(buf[BLK * q:BLK * q + BLK, :].rearrange("r (k e) -> r k e", k=2),
                                 w_mem[r0:r0 + 2 * BLK, :].rearrange("(k r) e -> r k e", k=2)).then_inc(done, DMA)
                elif kind in ("g1", "g2"):
                    g, h = g_piece(kind, i)
                    col = (D if kind == "g2" else 0) + DQ * q + PART * h
                    sp.dma_start(on_stage(buf, q, 8), blocks(w_gate, 256 * g, 256, col, PART)).then_inc(done, DMA)
                elif kind == "wt":
                    sp.dma_start(on_stage(buf, q, 8), blocks(w_mem, 256 * i, 256, EQ * q, EQ)).then_inc(done, DMA)
                elif kind == "ct":
                    sp.dma_start(on_stage(buf, q, 8), blocks(ctx_in[0], 0, M, EQ * q, EQ)).then_inc(done, DMA)
                else:
                    sp.dma_start(on_stage(buf, q, 4),
                                 blocks(x[0], PART * i, PART, DQ * q, DQ)).then_inc(done, DMA)

        def g_piece(kind, i):
            return (i // 2, i % 2) if kind == "g2" else (i % 4, i // 4)

        def turn_views(src, dst, i_count):
            k = D // (i_count * BLK)
            return (src[:, :].rearrange("p (i k r) -> p k i r", i=i_count, k=k),
                    dst[:, :].rearrange("p (k i c) -> p k i c", k=k, i=i_count))

        def halves(n, *views):
            if n > 1:
                return [(False, views)]
            k = views[0].shape[1] // 2
            return [(True, [v[:, :k] for v in views]), (False, [v[:, k:] for v in views])]

        def item_parts(n):
            kind, i = items[n]
            src = turned_bufs[turned_buf(n)]
            if kind == "wn":
                return (ring[n % 4][:, :].rearrange("p (k e) -> p k e", k=2),
                        wn_h[:, 2 * i:2 * i + 2, :], wn_l[:, 2 * i:2 * i + 2, :])
            if kind == "xt":
                v = src[:, :].rearrange("p (k n) -> p k n", k=KD)
                return v, xt_h[:, :, PART * i:PART * i + PART], xt_l[:, :, PART * i:PART * i + PART]
            v = src[:, :].rearrange("p (k n) -> p k n", k=4)
            if kind == "g2":
                return v, g2_h[:, i % 2], g2_l[:, i % 2]
            if kind == "wt":
                return (src[:, :].rearrange("p (e k r) -> p e k r", e=KE, k=KD),
                        *(w[:, :, :].rearrange("p e (k q r) -> p e k q r", k=KD, q=QUADS)[:, :, :, i, :]
                          for w in (wt_h, wt_l)))
            if kind == "ct":
                return v, ct_h[:, :, :], ct_l[:, :, :]
            g, h = g_piece(kind, i)
            return (v, g1_h[:, 4 * h:4 * h + 4, 256 * g:256 * g + 256],
                    g1_l[:, 4 * h:4 * h + 4, 256 * g:256 * g + 256])

        def p_tile(t):
            return t // 2, t % 2, (0, 1, 4, 5)[t]

        def p_cols(buf, mb, j):
            return buf[:, mb, BANK * j:BANK * j + BANK]

        PT_PARTS = [(0, slice(0, KD)), (1, slice(0, KD // 2)), (1, slice(KD // 2, KD))]

        def pt_part(buf, mb, chunks):
            return buf[:, chunks, PART * mb:PART * mb + PART]

        def p_natural(buf, mb, half):
            return buf[:, mb, :].rearrange("p (k q r) -> p q k r", k=KD, q=QUADS)[:, 2 * half:2 * half + 2]

        HALF = [slice(BANK * half, BANK * half + BANK) for half in range(HALVES)]
        BLOCKS_BEFORE = NB * B - 1
        block = ctx.enter_context(nc.Block())

        @block.sync
        def _(sp):
            for n in range(4):
                load_item(sp, n)
            for n in range(4, len(items)):
                if items[n - 4][0] == "wn":
                    sp.wait_ge(*is_cut(n - 4))
                else:
                    sp.wait_ge(item_turned, turned_count(n - 4))
                load_item(sp, n)
            sp.dma_start(bias[:, :], b_gate.rearrange("(a d) -> a d", a=1).to_broadcast((PART, D))
                         ).then_inc(consts_in, DMA)

            def load_c_rows(b, first):
                if first:
                    sp.wait_ge(item_turned, turned_count(max(range(0, len(items), 4))))
                else:
                    sp.wait_ge(xs_moved, 2 * b)
                sp.dma_start(stage[:, :].rearrange("p (m e) -> p m e", m=MB),
                             ctx_in[bass.ds(b, 1)].rearrange("a (m p) e -> p (a m) e", p=PART)).then_inc(cn_in, DMA)

            def rows_of(array, b, nb):
                return array[bass.ds(b, 1), PART * nb:PART * nb + PART, :].rearrange("a p d -> p (a d)")

            def load_x_rows(b, nb):
                sp.dma_start(xrow[nb][:, :], rows_of(x, b, nb)).then_inc(xrow_in[nb], DMA)

            def store_rows(b, nb):
                sp.wait_ge(row_ready, 2 * b + nb + 1)
                sp.dma_start(rows_of(out, b, nb), xrow[nb][:, :]).then_inc(out_done[nb], DMA)

            def batch(b, first):
                for nb in range(NB):
                    if nb == 1:
                        sp.wait_ge(cn_ready, b)
                    elif first:
                        sp.wait_ge(item_turned, turned_count(len(items) - 1))
                    else:
                        sp.wait_ge(f_ready, 2 * (b - 1))
                    for q in range(QUADS):
                        sp.dma_start(on_stage((gate, stage)[nb], q, 4),
                                     x[bass.ds(b, 1), PART * nb:PART * nb + PART, DQ * q:DQ * q + DQ].rearrange(
                                         "a (i c) f -> c (a i) f", c=BLK)).then_inc(xs_in[nb], DMA)
                if not first:
                    store_rows(b - 2, 1)
                sp.wait_ge(xs_moved, 2 * b - 1)
                for q in range(QUADS):
                    sp.dma_start(on_stage(gate, q, 8),
                                 ctx_in[bass.ds(b, 1), :, EQ * q:EQ * q + EQ].rearrange(
                                     "a (i c) f -> c (a i) f", c=BLK)).then_inc(cs_in, DMA)
                if not first:
                    sp.wait_ge(out_done[1], DMA * (b - 1))
                load_c_rows(b, False)
                store_rows(b - 1, 0)
                if not first:
                    load_x_rows(b - 1, 1)
                sp.wait_ge(out_done[0], DMA * b)
                load_x_rows(b, 0)

            sp.wait_ge(*is_cut(pos["g1", 5]))
            sp.dma_start(norm[:, :], norm_w.rearrange("(a d) -> a d", a=1).to_broadcast((PART, D))
                         ).then_inc(consts_in, DMA)
            load_c_rows(0, True)
            sp.wait_ge(item_turned, turned_count(len(items) - 1))
            for nb in range(NB):
                load_x_rows(0, nb)
            batch(1, True)
            with sp.Fori(2, B) as b:
                batch(b, False)
            store_rows(B - 2, 1)
            sp.wait_ge(out_done[1], DMA * (B - 1))
            load_x_rows(B - 1, 1)
            store_rows(B - 1, 0)
            for half in range(HALVES):
                sp.wait_ge(row_ready, BLOCKS_BEFORE + half + 1)
                sp.dma_start(out[B - 1, N - PART:N, HALF[half]], xrow[NB - 1][:, HALF[half]]
                             ).then_inc(out_done[NB - 1], DMA)
            for nb in range(NB):
                sp.wait_ge(out_done[nb], DMA * (B + nb * (HALVES - 1)))

        @block.gpsimd
        def _(pool):
            pool.memset(minus_half, -0.5).then_inc(consts_done, 1)
            pool.memset(eps, EPS).then_inc(consts_done, 1)
            pool.wait_ge(consts_done, 2)
            for n, item in enumerate(items):
                if item in POOL_ITEMS:
                    src, high, lo = item_parts(n)
                    pool.wait_ge(item_h, n + 1)
                    if item[0] == "g1":
                        pool.wait_ge(g2_used, 8)
                    pool.tensor_tensor(lo, src, high.bitcast(F32), ALU.subtract).then_inc(item_low_pool, 1)

            def batch(b, n_blocks=NB):
                pool.wait_ge(cn_high, b + 1)
                pool.tensor_tensor(ctt_l[:, :, :].rearrange("p j (m c) -> p j m c", m=MB),
                                   stage[:, :].rearrange("p (m j c) -> p j m c", m=MB, j=KE),
                                   ctt_h[:, :, :].rearrange("p j (m c) -> p j m c", m=MB).bitcast(F32),
                                   ALU.subtract).then_inc(cn_ready, 1)
                for nb in range(n_blocks):
                    done = 2 * b + nb + 1
                    pool.wait_ge(sq_done, done)
                    pool.tensor_tensor(guarded[:, nb:nb + 1], meansq[:, nb:nb + 1], eps,
                                       ALU.add).then_inc(guarded_done, 1)
                    pool.wait_ge(guarded_done, done)
                    pool.tensor_tensor(rstd[:, nb:nb + 1], guarded[:, nb:nb + 1], minus_half,
                                       ALU.pow).then_inc(rstd_ready, 1)

            batch(0)
            with pool.Fori(1, B - 1) as b:
                batch(b)
            batch(B - 1, NB - 1)
            pool.wait_ge(sq_done, BLOCKS_BEFORE + 1)
            pool.tensor_tensor(half_sq[:, 0:1], half_sq[:, 0:1], eps, ALU.add).then_inc(guarded_done, 1)
            pool.wait_ge(guarded_done, BLOCKS_BEFORE + 1)
            pool.wait_ge(sq_done, BLOCKS_BEFORE + 2)
            pool.tensor_tensor(guarded[:, 1:2], half_sq[:, 0:1], half_sq[:, 1:2], ALU.add).then_inc(guarded_done, 1)
            pool.wait_ge(guarded_done, BLOCKS_BEFORE + 2)
            pool.tensor_tensor(rstd[:, 1:2], guarded[:, 1:2], minus_half, ALU.pow).then_inc(rstd_ready, 1)

        @block.scalar
        def _(act):
            def copy(dst, src):
                return nc.scalar.activation(dst, src, ACT.Copy)

            def item(n):
                kind, i = items[n]
                src, high, _ = item_parts(n)
                if kind == "wn":
                    act.wait_ge(ring_in[n % 4], ring_count(n))
                elif n > 1:
                    act.wait_ge(item_turned, turned_count(n))
                if kind == "g2" and i >= 2:
                    act.wait_ge(g2_used, i - 1)
                for is_half, (high_part, src_part) in halves(n, high, src):
                    if n == 0:
                        act.wait_ge(half_turned if is_half else item_turned, 1)
                    copy(high_part, src_part).then_inc(half_h if is_half else item_h, 1)

            def k_part(g):
                act.wait_ge(g2_used, 2 * g + 2)
                copy(k_h[:, :, DQ * g:DQ * g + DQ],
                     psum[:, 4 * (g % 2):4 * (g % 2) + 4, 0:DQ]).then_inc(k_high, 1)

            for n in range(n_before_k):
                item(n)
                if items[n] in K_PARTS:
                    k_part(K_PARTS[items[n]])
            for i in range(4):
                item(pos["g1", i])
            k_part(3)

            def square(b, nb):
                act.wait_ge(f_ready, 2 * b + nb + 1)
                nc.scalar.activation(turned[:, :], xrow[nb][:, :], ACT.Square, scale=SCALE,
                                     accum_out=meansq[:, nb:nb + 1]).then_inc(sq_done, 1)

            def batch(b, first, last):
                for t in range(4):
                    mb, j, bk = p_tile(t)
                    act.wait_ge(p_mm, 4 * b + t + 1)
                    copy(p_cols(p_h, mb, j), bank(bk)).then_inc(p_high, 1)
                    if first and t == 1:
                        for i in range(4, 8):
                            item(pos["g1", i])
                for mb, chunks in PT_PARTS:
                    act.wait_ge(p_turned, 2 * b + mb + 1)
                    copy(pt_part(pt_h, mb, chunks), pt_part(pt32, mb, chunks)).then_inc(pt_high, 1)
                if not first:
                    square(b - 1, 1)
                act.wait_ge(negmax_done, b + 1)
                for nb in range(NB):
                    nc.scalar.activation(prob[:, nb, :], psum[:, 6 + nb, 0:M], ACT.Exp, bias=negmax[:, nb:nb + 1],
                                         scale=SCALE, accum_out=rowsum[:, nb:nb + 1]).then_inc(exp_done, 1)
                act.wait_ge(s_mm, b + 1)
                act.wait_ge(cn_in, DMA * (b + 1))
                copy(ctt_h[:, :, :].rearrange("p j (m c) -> p j m c", m=MB),
                     stage[:, :].rearrange("p (m j c) -> p j m c", m=MB, j=KE)).then_inc(cn_high, 1)
                act.wait_ge(at_turned, b + 1)
                copy(at_h[:, :, :], at32[:, :, :]).then_inc(at_high, 1)
                for i in range(2):
                    act.wait_ge(tt_mm, 2 * b + i + 1)
                    copy(ctt_h[:, 2 * i:2 * i + 2, :].rearrange("p j n -> p (j n)"),
                         bank(6 + i)).then_inc(tt_high, 1)
                if not last:
                    act.wait_ge(xt_used, b + 1)
                    for nb in range(NB):
                        act.wait_ge(xs_moved, 2 * b + nb + 1)
                        copy(xt_h[:, :, PART * nb:PART * nb + PART],
                             turned[:, :].rearrange("p (k n) -> p k n", k=KD)).then_inc(xt_high, 1)
                    act.wait_ge(cs_moved, b + 1)
                    act.wait_ge(m_mm, b + 1)
                    copy(ct_h[:, :, :], turned[:, :].rearrange("p (k n) -> p k n", k=KE)).then_inc(ct_high, 1)
                for nb in range(NB - 1 if last else NB):
                    done = 2 * b + nb + 1
                    act.wait_ge(z_ready, done)
                    nc.scalar.activation(gate[:, :], gate[:, :], ACT.Tanh, scale=0.5).then_inc(tanh_done, 1)
                    if nb == 0:
                        square(b, 0)

            batch(0, True, False)
            with act.Fori(1, B - 1) as b:
                batch(b, False, False)
            batch(B - 1, False, True)

            def tanh_half(half):
                act.wait_ge(z_ready, BLOCKS_BEFORE + half + 1)
                nc.scalar.activation(stage[:, HALF[half]], stage[:, HALF[half]], ACT.Tanh, scale=0.5
                                     ).then_inc(tanh_done, 1)

            def square_half(half):
                act.wait_ge(f_ready, BLOCKS_BEFORE + half + 1)
                nc.scalar.activation(turned[:, HALF[half]], xrow[NB - 1][:, HALF[half]], ACT.Square, scale=SCALE,
                                     accum_out=half_sq[:, half:half + 1]).then_inc(sq_done, 1)

            tanh_half(0)
            act.wait_ge(sq_done, BLOCKS_BEFORE)
            square_half(0)
            tanh_half(1)
            square_half(1)

        @block.vector
        def _(dve):
            def low(dst, src, high):
                return nc.vector.tensor_tensor(dst, src, high.bitcast(F32), ALU.subtract)

            def turn(n):
                kind, i = items[n]
                dve.wait_ge(ring_in[n % 4], ring_count(n))
                before = [m for m in range(n) if items[m][0] != "wn" and turned_buf(m) == turned_buf(n)]
                if before:
                    dve.wait_ge(*is_cut(before[-1]))
                src, dst = turn_views(ring[n % 4], turned_bufs[turned_buf(n)], 4 if kind == "xt" else 8)
                for is_half, (dst_part, src_part) in halves(n, dst, src):
                    nc.vector.transpose(dst_part, src_part).then_inc(half_turned if is_half else item_turned, 1)

            def cut(n):
                kind, i = items[n]
                src, high, lo = item_parts(n)
                if kind == "g1":
                    dve.wait_ge(g2_used, 8)
                for is_half, (lo_part, src_part, high_part) in halves(n, lo, src, high):
                    dve.wait_ge(half_h if is_half else item_h, n + 1)
                    low(lo_part, src_part, high_part).then_inc(half_low if is_half else item_low, 1)

            def k_part(g):
                dve.wait_ge(k_high, g + 1)
                cols = slice(DQ * g, DQ * g + DQ)
                low(k_l[:, :, cols], psum[:, 4 * (g % 2):4 * (g % 2) + 4, 0:DQ], k_h[:, :, cols]).then_inc(k_ready, 1)

            turn(0)
            for n in range(n_before_k):
                if n + 1 < n_before_k and items[n + 1][0] != "wn":
                    turn(n + 1)
                if items[n] not in POOL_ITEMS:
                    cut(n)
                if items[n] in K_PARTS:
                    k_part(K_PARTS[items[n]])
            for i in range(4):
                turn(pos["g1", i])
            cut(pos["g1", 0])
            k_part(3)
            cut(pos["g1", 2])

            def scale_rows(b, nb):
                dve.wait_ge(rstd_ready, 2 * b + nb + 1)
                nc.vector.scalar_tensor_tensor(xrow[nb][:, :], xrow[nb][:, :], rstd[:, nb:nb + 1], norm[:, :],
                                               ALU.mult, ALU.mult).then_inc(row_ready, 1)

            def turn_p(b, mb):
                tile = psum[:, 4 * mb:4 * mb + 2, :].rearrange("p j (k q c) -> p (j k) q c", q=QUADS, c=BLK)
                for qm in range(QUADS):
                    col = PART * mb + BLK * qm
                    for q in range(QUADS):
                        last = nc.vector.transpose(pt32[BLK * q:BLK * q + BLK, :, col:col + BLK],
                                                   tile[BLK * qm:BLK * qm + BLK, :, q, :])
                last.then_inc(p_turned, 1)

            def turn_a():
                for qn in range(QUADS):
                    for q in range(QUADS):
                        last = nc.vector.transpose(
                            at32.rearrange("p m (n q c) -> p n m q c", q=QUADS, c=BLK)[BLK * q:BLK * q + BLK, :, :, qn, :],
                            prob.rearrange("p n (m q c) -> p n m q c", q=QUADS, c=BLK)[BLK * qn:BLK * qn + BLK, :, :, q, :])
                last.then_inc(at_turned, 1)

            def add_rows(b, nb):
                dve.wait_ge(gm_ready, 2 * b + nb + 1)
                dve.wait_ge(xrow_in[nb], DMA * (b + 1))
                nc.vector.scalar_tensor_tensor(xrow[nb][:, :], gate[:, :], 0.5, xrow[nb][:, :],
                                               ALU.mult, ALU.add).then_inc(f_ready, 1)

            def cut_p(b, mb):
                for t in (2 * mb, 2 * mb + 1):
                    j, bk = p_tile(t)[1:]
                    low(p_cols(p_l, mb, j), bank(bk), p_cols(p_h, mb, j)).then_inc(p_ready, 1)

            def cut_pt(b, part):
                mb, chunks = PT_PARTS[part]
                dve.wait_ge(pt_high, len(PT_PARTS) * b + part + 1)
                low(pt_part(pt_l, mb, chunks), pt_part(pt32, mb, chunks), pt_part(pt_h, mb, chunks)
                    ).then_inc(pt_ready, 1)

            def batch(b, first, last):
                if first:
                    for i in range(4):
                        turn(pos["g1", 4 + i])
                    cut(pos["g1", 6])
                    cut(pos["g1", 7])
                    for i in (2, 3, 6, 7):
                        dve.wait_ge(*is_cut(pos["g1", i]))
                dve.wait_ge(p_high, 4 * b + 2)
                turn_p(b, 0)
                cut_p(b, 0)
                cut_pt(b, 0)
                dve.wait_ge(p_high, 4 * b + 4)
                turn_p(b, 1)
                cut_pt(b, 1)
                cut_pt(b, 2)
                cut_p(b, 1)
                if not first:
                    add_rows(b - 1, 1)
                dve.wait_ge(s_mm, b + 1)
                nc.vector.tensor_reduce(rowmax, psum[:, 6:8, 0:M], AX.X, ALU.max).then_inc(max_done, 1)
                dve.wait_ge(max_done, b + 1)
                nc.vector.tensor_scalar(negmax, rowmax, -SCALE, None, ALU.mult).then_inc(negmax_done, 1)
                dve.wait_ge(exp_done, 2 * b + 2)
                nc.vector.reciprocal(rowinv, rowsum).then_inc(inv_done, 1)
                dve.wait_ge(inv_done, b + 1)
                for nb in range(NB):
                    nc.vector.tensor_scalar(prob[:, nb, :], prob[:, nb, :], rowinv[:, nb:nb + 1], None,
                                            ALU.mult).then_inc(prob_ready, 1)
                dve.wait_ge(prob_ready, 2 * b + 2)
                turn_a()
                dve.wait_ge(at_high, b + 1)
                low(at_l[:, :, :], at32[:, :, :], at_h[:, :, :]).then_inc(at_ready, 1)
                if not first:
                    scale_rows(b - 1, 1)

                def turn_x(nb):
                    dve.wait_ge(xs_in[nb], DMA * QUADS * (b + 1))
                    src, dst = turn_views((gate, stage)[nb], turned, 4)
                    nc.vector.transpose(dst, src).then_inc(xs_moved, 1)

                if not last:
                    if first:
                        dve.wait_ge(*is_cut(pos["g1", 4]))
                    else:
                        dve.wait_ge(ct_ready, b)
                    turn_x(0)
                for i in range(2):
                    dve.wait_ge(tt_high, 2 * b + i + 1)
                    rows = slice(2 * i, 2 * i + 2)
                    low(ctt_l[:, rows, :].rearrange("p j n -> p (j n)"), bank(6 + i),
                        ctt_h[:, rows, :].rearrange("p j n -> p (j n)")).then_inc(tt_ready, 1)
                if not last:
                    for nb in range(NB):
                        if nb == 1:
                            dve.wait_ge(xt_ready, 2 * b + 1)
                            turn_x(1)
                        dve.wait_ge(xt_high, 2 * b + nb + 1)
                        cols = slice(PART * nb, PART * nb + PART)
                        low(xt_l[:, :, cols], turned[:, :].rearrange("p (k n) -> p k n", k=KD),
                            xt_h[:, :, cols]).then_inc(xt_ready, 1)
                    dve.wait_ge(xt_ready, 2 * b + 2)
                    dve.wait_ge(cs_in, DMA * QUADS * (b + 1))
                    src, dst = turn_views(gate, turned, 8)
                    nc.vector.transpose(dst, src).then_inc(cs_moved, 1)
                    dve.wait_ge(ct_high, b + 1)
                    low(ct_l[:, :, :], turned[:, :].rearrange("p (k n) -> p k n", k=KE),
                        ct_h[:, :, :]).then_inc(ct_ready, 1)
                if first:
                    dve.wait_ge(consts_in, 2 * DMA)
                for nb in range(NB - 1 if last else NB):
                    done = 2 * b + nb + 1
                    dve.wait_ge(gate_mm, done)
                    if nb == 1:
                        dve.wait_ge(f_ready, done - 1)
                    nc.vector.tensor_tensor(gate[:, :], psum[:, 2 * nb:2 * nb + 2, :].rearrange("p h c -> p (h c)"),
                                            bias[:, :], ALU.add).then_inc(z_ready, 1)
                    if nb == 1:
                        scale_rows(b, 0)
                    dve.wait_ge(tanh_done, done)
                    nc.vector.scalar_tensor_tensor(
                        gate[:, :], gate[:, :], 1.0, psum[:, 4 + 2 * nb:6 + 2 * nb, :].rearrange("p h c -> p (h c)"),
                        ALU.add, ALU.mult).then_inc(gm_ready, 1)
                    if nb == 0:
                        add_rows(b, 0)

            batch(0, True, False)
            with dve.Fori(1, B - 1) as b:
                batch(b, False, False)
            batch(B - 1, False, True)

            nb = NB - 1

            def add_bias(half):
                dve.wait_ge(gate_mm, BLOCKS_BEFORE + half + 1)
                nc.vector.tensor_tensor(stage[:, HALF[half]], bank(2 * nb + half), bias[:, HALF[half]],
                                        ALU.add).then_inc(z_ready, 1)

            def gated_sum(half):
                count = BLOCKS_BEFORE + half + 1
                dve.wait_ge(tanh_done, count)
                nc.vector.scalar_tensor_tensor(stage[:, HALF[half]], stage[:, HALF[half]], 1.0,
                                               bank(4 + 2 * nb + half), ALU.add, ALU.mult).then_inc(gm_ready, 1)
                dve.wait_ge(gm_ready, count)
                dve.wait_ge(xrow_in[nb], DMA * B)
                nc.vector.scalar_tensor_tensor(xrow[nb][:, HALF[half]], stage[:, HALF[half]], 0.5,
                                               xrow[nb][:, HALF[half]], ALU.mult, ALU.add).then_inc(f_ready, 1)

            dve.wait_ge(cn_ready, B)
            add_bias(0)
            gated_sum(0)
            add_bias(1)
            gated_sum(1)
            scale_rows(B - 1, 0)
            dve.wait_ge(rstd_ready, NB * B)
            for half in range(HALVES):
                nc.vector.scalar_tensor_tensor(xrow[nb][:, HALF[half]], xrow[nb][:, HALF[half]], rstd[:, nb:nb + 1],
                                               norm[:, HALF[half]], ALU.mult, ALU.mult).then_inc(row_ready, 1)

        @block.tensor
        def _(pe):
            def product(tiles, pairs, start=True, stop=True):
                last = [None] * len(tiles)
                for i, ((ah, al), moving) in enumerate(pairs):
                    for tile, (mh, ml) in zip(tiles, moving):
                        nc.tensor.matmul(tile, ah, mh, start=start and i == 0, stop=False)
                        nc.tensor.matmul(tile, ah, ml, start=False, stop=False)
                    for t, (tile, (mh, ml)) in enumerate(zip(tiles, moving)):
                        last[t] = nc.tensor.matmul(tile, al, mh, start=False, stop=stop and i == len(pairs) - 1)
                return last

            for g in range(4):
                if g >= 2:
                    pe.wait_ge(k_ready, g - 1)
                for h in range(2):
                    for n in range(4):
                        first_piece = g == 0 and h == 0
                        if n == (1 if first_piece else 0):
                            pe.wait_ge(*is_cut(pos["g2", 2 * g + h]))
                        if first_piece and n == 0:
                            pe.wait_ge(half_low, 2)
                        elif g == 0 and (n % 2 == 0 or n == 1 and first_piece):
                            pe.wait_ge(*is_cut(pos["wn", (4 * h + n) // 2]))
                        kd = 4 * h + n
                        for e in range(KE):
                            cols = slice(PART * e, PART * e + PART)
                            last = product([psum[:, 4 * (g % 2) + e, 0:DQ]],
                                           [((wn_h[:, kd, cols], wn_l[:, kd, cols]),
                                             [(g2_h[:, h, n, :], g2_l[:, h, n, :])])],
                                           start=kd == 0, stop=kd == KD - 1)
                    last[0].then_inc(g2_used, 1)

            def batch(b, first, last_batch):
                if first:
                    for i in range(4):
                        pe.wait_ge(*is_cut(pos["wt", i]))
                    pe.wait_ge(*is_cut(pos["ct", 0]))
                else:
                    pe.wait_ge(ct_ready, b)
                for mb in range(MB):
                    if first:
                        pe.wait_ge(k_ready, 3 + mb)
                    elif mb == 0:
                        pe.wait_ge(z_ready, 2 * b - 1)
                    else:
                        pe.wait_ge(gm_ready, 2 * b - 1)
                    rows = slice(PART * mb, PART * mb + PART)
                    tiles = [bank(p_tile(2 * mb + j)[2]) for j in range(2)]
                    for last in product(tiles, [((ct_h[:, k, rows], ct_l[:, k, rows]),
                                                 [(wt_h[:, k, cols], wt_l[:, k, cols]) for cols in HALF])
                                                for k in range(KE)]):
                        last.then_inc(p_mm, 1)

                def gate_x(nb, k0, k1):
                    rows = slice(PART * nb, PART * nb + PART)
                    return product([bank(2 * nb), bank(2 * nb + 1)],
                                   [((xt_h[:, k, rows], xt_l[:, k, rows]),
                                     [(g1_h[:, k, cols], g1_l[:, k, cols]) for cols in HALF])
                                    for k in range(k0, k1)], start=k0 == 0, stop=False)[-1]

                if first:
                    for i in range(4):
                        pe.wait_ge(*is_cut(pos["g1", i]))
                    pe.wait_ge(*is_cut(pos["xt", 1]))
                else:
                    pe.wait_ge(xt_ready, 2 * b)
                    pe.wait_ge(z_ready, 2 * b)
                gate_x(1, 0, 4)
                if first:
                    for i in range(4, 8):
                        pe.wait_ge(*is_cut(pos["g1", i]))
                gate_x(1, 4, KD)
                pe.wait_ge(p_ready, 4 * b + 2)
                before_s = 3 if first else 2
                gate_x(0, 0, before_s)

                if not first:
                    pe.wait_ge(gm_ready, 2 * b)
                for k in range(KD):
                    if k % 4 == 0:
                        pe.wait_ge(pt_ready, len(PT_PARTS) * b + k // 4 + 2)
                    for nb in range(NB):
                        rows = slice(PART * nb, PART * nb + PART)
                        last = product([psum[:, 6 + nb, 0:M]],
                                       [((xt_h[:, k, rows], xt_l[:, k, rows]), [(pt_h[:, k, :], pt_l[:, k, :])])],
                                       start=k == 0, stop=k == KD - 1)
                last[0].then_inc(s_mm, 1)
                gate_x(0, before_s, KD).then_inc(xt_used, 1)

                pe.wait_ge(cn_ready, b + 1)
                pe.wait_ge(at_ready, b + 1)
                for j in range(KE):
                    last = product([bank(6 + j // 2)[:, N * (j % 2):N * (j % 2) + N]],
                                   [((ctt_h[:, j, PART * mb:PART * mb + PART], ctt_l[:, j, PART * mb:PART * mb + PART]),
                                     [(at_h[:, mb, :], at_l[:, mb, :])]) for mb in range(MB)])
                    if j % 2:
                        last[0].then_inc(tt_mm, 1)

                def memory(nb):
                    rows = slice(PART * nb, PART * nb + PART)
                    if nb == 1:
                        pe.wait_ge(tt_ready, 2 * b + 2)
                    return product([bank(4 + 2 * nb), bank(5 + 2 * nb)],
                                   [((at_h[:, mb, rows], at_l[:, mb, rows]),
                                     [(p_natural(p_h, mb, half), p_natural(p_l, mb, half)) for half in range(HALVES)])
                                    for mb in range(MB)])[-1]

                def gate_m(nb, halves):
                    rows = slice(PART * nb, PART * nb + PART)
                    return product([bank(2 * nb + half) for half in halves],
                                   [((ctt_h[:, j, rows], ctt_l[:, j, rows]),
                                     [(k_h[:, j, HALF[half]], k_l[:, j, HALF[half]]) for half in halves])
                                    for j in range(KE)], start=False)[-1]

                pe.wait_ge(p_ready, 4 * b + 4)
                memory(0)
                if not last_batch:
                    memory(1).then_inc(m_mm, 1)
                    gate_m(0, (0, 1)).then_inc(gate_mm, 1)
                    gate_m(1, (0, 1)).then_inc(gate_mm, 1)
                else:
                    pe.wait_ge(tt_ready, 2 * b + 2)
                    gate_m(0, (0, 1)).then_inc(gate_mm, 1)
                    memory(1)
                    gate_m(1, (0,)).then_inc(gate_mm, 1)
                    gate_m(1, (1,)).then_inc(gate_mm, 1)

            batch(0, True, False)
            with pe.Fori(1, B - 1) as b:
                batch(b, False, False)
            batch(B - 1, False, True)


_INS = ["x", "ctx_1024", "L0_xattn_W_mem", "L0_xattn_W_gate", "L0_xattn_b_gate", "L0_xattn_norm_w"]


def kernel(**inputs):
    import concourse.bacc as bacc
    import numpy as np
    from concourse.bass_utils import run_bass_kernel_spmd

    nc = bacc.Bacc("TRN2", target_bir_lowering=False, num_devices=1)
    arrays, args = {}, []
    for name in _INS:
        a = np.ascontiguousarray(inputs[name])
        arrays[f"in_{name}"] = a
        args.append(nc.dram_tensor(f"in_{name}", a.shape, mybir.dt.from_np(a.dtype), kind="ExternalInput").ap())
    args.append(nc.dram_tensor("out_0", inputs["x"].shape, F32, kind="ExternalOutput").ap())
    build(nc, *args)
    result = run_bass_kernel_spmd(nc, [arrays], core_ids=[0])
    return result.results[0]["out_0"]
```
